# Optimizing a Trainium2 kernel written in Bass

```python
import numpy as np
import jax
import jax.numpy as jnp

def _softmax(x, axis=-1):
    return jax.nn.softmax(x, axis=axis)

def _gelu(x):
    return jax.nn.gelu(x, approximate=True)

def _silu(x):
    return jax.nn.silu(x)

def _sigmoid(x):
    return jax.nn.sigmoid(x)

def _layernorm(x, axis=-1, eps=1e-05):
    m = jnp.mean(x, axis=axis, keepdims=True)
    v = jnp.var(x, axis=axis, keepdims=True)
    return (x - m) / jnp.sqrt(v + eps)

def _scatter_add(tgt, idx, src, axis=0):
    return tgt.at[idx].add(src)

def _segment_sum(src, seg, n):
    return jax.ops.segment_sum(src, seg, n)
kernel_name = 'mk_seq_postln_d2_jaxref_r8_fd3b53'

def setup_inputs(seed: int=0):
    np.random.seed(seed)
    _w = jnp.asarray

    def _L0_attn_setup():
        import jax, jax.numpy as jnp
        import numpy as np
        EPS = 1e-06
        key = jax.random.key(seed)
        kx, kw = jax.random.split(key)
        B, L, D = (4, 1024, 128)
        x = jax.random.normal(kx, (B, L, D), dtype=jnp.float32)
        W = jax.random.normal(kw, (D, 3 * D), dtype=jnp.float32) * 0.02
        return {'x': x, 'W': W}
    _L0_attn_in = _L0_attn_setup()

    def _L0_ffn_setup():
        import jax, jax.numpy as jnp
        import numpy as np
        E = 32
        K = 4
        H = 128
        I = 64
        B, S = (2, 256)
        T = B * S
        C = 128
        ROUTED_SCALE = 1.0

        def _silu_and_mul(gu):
            g, u = jnp.split(gu, 2, axis=-1)
            return jax.nn.silu(g) * u
        key = jax.random.key(seed)
        ks = jax.random.split(key, 6)
        s = 0.02
        return {'hidden_states': jax.random.normal(ks[0], (B, S, H), jnp.float32), 'gate_w': jax.random.normal(ks[1], (E, H), jnp.float32) * s, 'w_gate_up': jax.random.normal(ks[2], (E, H, 2 * I), jnp.float32) * s, 'w_down': jax.random.normal(ks[3], (E, I, H), jnp.float32) * s, 'shared_w_gate_up': jax.random.normal(ks[4], (H, 2 * I), jnp.float32) * s, 'shared_w_down': jax.random.normal(ks[5], (I, H), jnp.float32) * s}
    _L0_ffn_in = _L0_ffn_setup()

    def _L1_attn_setup():
        import jax, jax.numpy as jnp
        import numpy as np
        D_MODEL, D_STATE, D_CONV, EXPAND = (128, 16, 4, 2)
        D_INNER = EXPAND * D_MODEL
        BATCH, SEQ = (1, 512)

        def _selective_ssm(x, x_proj_w, dt_proj_w, dt_proj_b, A_log, D):
            xp = x @ x_proj_w.T
            dt_raw = xp[..., :1]
            B = xp[..., 1:D_STATE + 1]
            C = xp[..., D_STATE + 1:]
            dt = jax.nn.softplus(dt_raw @ dt_proj_w.T + dt_proj_b)
            A = -jnp.exp(A_log)
            dA = jnp.exp(jnp.einsum('bld,dn->bldn', dt, A))
            dBx = (dt * x)[..., None] * B[:, :, None, :]

            def step(h, inp):
                dA_t, dBx_t, C_t = inp
                h = dA_t * h + dBx_t
                y = jnp.einsum('bdn,bn->bd', h, C_t)
                return (h, y)
            h0 = jnp.zeros((x.shape[0], D_INNER, D_STATE), x.dtype)
            _, ys = jax.lax.scan(step, h0, (dA.transpose(1, 0, 2, 3), dBx.transpose(1, 0, 2, 3), C.transpose(1, 0, 2)))
            y = ys.transpose(1, 0, 2)
            return y + x * D
        key = jax.random.key(seed)
        ks = jax.random.split(key, 8)
        s_in = 1.0 / np.sqrt(D_MODEL)
        s_xi = 1.0 / np.sqrt(D_INNER)
        A_log = jnp.log(jnp.tile(jnp.arange(1, D_STATE + 1, dtype=jnp.float32)[None, :], (D_INNER, 1)))
        return {'x': jax.random.normal(ks[0], (BATCH, SEQ, D_MODEL), jnp.float32), 'in_proj_w': jax.random.normal(ks[1], (2 * D_INNER, D_MODEL), jnp.float32) * s_in, 'conv_w': jax.random.normal(ks[2], (D_INNER, 1, D_CONV), jnp.float32) * 0.5, 'conv_b': jnp.zeros((D_INNER,), jnp.float32), 'x_proj_w': jax.random.normal(ks[3], (2 * D_STATE + 1, D_INNER), jnp.float32) * s_xi, 'dt_proj_w': jax.random.normal(ks[4], (D_INNER, 1), jnp.float32), 'dt_proj_b': jax.random.normal(ks[5], (D_INNER,), jnp.float32) * 0.1, 'A_log': A_log, 'D': jnp.ones((D_INNER,), jnp.float32), 'out_proj_w': jax.random.normal(ks[6], (D_MODEL, D_INNER), jnp.float32) * s_xi}
    _L1_attn_in = _L1_attn_setup()

    def _L1_ffn_setup():
        import jax, jax.numpy as jnp
        import numpy as np
        from jax import lax
        D = 128
        H = 176
        E = 8
        K = 2
        ROUTER_SCALE = 1.0

        def _expert(x, w1, b1, w3, b3, w2, b2):
            h = jax.nn.silu((x @ w1 + b1) * (x @ w3 + b3))
            return h @ w2 + b2
        key = jax.random.key(seed)
        ks = jax.random.split(key, 16)
        s = 0.02
        inp = {'x': jax.random.normal(ks[0], (2, 256, D), dtype=jnp.float32), 'gate_w': jax.random.normal(ks[1], (E, D), dtype=jnp.float32) * s, 'gate_b': jax.random.normal(ks[2], (E,), dtype=jnp.float32) * s, 'w1': jax.random.normal(ks[3], (E, D, H), dtype=jnp.float32) * s, 'b1': jax.random.normal(ks[4], (E, H), dtype=jnp.float32) * s, 'w3': jax.random.normal(ks[5], (E, D, H), dtype=jnp.float32) * s, 'b3': jax.random.normal(ks[6], (E, H), dtype=jnp.float32) * s, 'w2': jax.random.normal(ks[7], (E, H, D), dtype=jnp.float32) * s, 'b2': jax.random.normal(ks[8], (E, D), dtype=jnp.float32) * s, 'sw1': jax.random.normal(ks[9], (D, H), dtype=jnp.float32) * s, 'sb1': jax.random.normal(ks[10], (H,), dtype=jnp.float32) * s, 'sw3': jax.random.normal(ks[11], (D, H), dtype=jnp.float32) * s, 'sb3': jax.random.normal(ks[12], (H,), dtype=jnp.float32) * s, 'sw2': jax.random.normal(ks[13], (H, D), dtype=jnp.float32) * s, 'sb2': jax.random.normal(ks[14], (D,), dtype=jnp.float32) * s}
        return inp
    _L1_ffn_in = _L1_ffn_setup()
    _d = {'L0_attn_x': _L0_attn_in['x'], 'L0_attn_W': _L0_attn_in['W'], 'L0_ffn_gate_w': _L0_ffn_in['gate_w'], 'L0_ffn_w_gate_up': _L0_ffn_in['w_gate_up'], 'L0_ffn_w_down': _L0_ffn_in['w_down'], 'L0_ffn_shared_w_gate_up': _L0_ffn_in['shared_w_gate_up'], 'L0_ffn_shared_w_down': _L0_ffn_in['shared_w_down'], 'L1_attn_in_proj_w': _L1_attn_in['in_proj_w'], 'L1_attn_conv_w': _L1_attn_in['conv_w'], 'L1_attn_conv_b': _L1_attn_in['conv_b'], 'L1_attn_x_proj_w': _L1_attn_in['x_proj_w'], 'L1_attn_dt_proj_w': _L1_attn_in['dt_proj_w'], 'L1_attn_dt_proj_b': _L1_attn_in['dt_proj_b'], 'L1_attn_A_log': _L1_attn_in['A_log'], 'L1_attn_D': _L1_attn_in['D'], 'L1_attn_out_proj_w': _L1_attn_in['out_proj_w'], 'L1_ffn_gate_w': _L1_ffn_in['gate_w'], 'L1_ffn_gate_b': _L1_ffn_in['gate_b'], 'L1_ffn_w1': _L1_ffn_in['w1'], 'L1_ffn_b1': _L1_ffn_in['b1'], 'L1_ffn_w3': _L1_ffn_in['w3'], 'L1_ffn_b3': _L1_ffn_in['b3'], 'L1_ffn_w2': _L1_ffn_in['w2'], 'L1_ffn_b2': _L1_ffn_in['b2'], 'L1_ffn_sw1': _L1_ffn_in['sw1'], 'L1_ffn_sb1': _L1_ffn_in['sb1'], 'L1_ffn_sw3': _L1_ffn_in['sw3'], 'L1_ffn_sb3': _L1_ffn_in['sb3'], 'L1_ffn_sw2': _L1_ffn_in['sw2'], 'L1_ffn_sb2': _L1_ffn_in['sb2']}
    _x0 = _d['L0_attn_x']
    _d['L0_attn_x'] = jax.random.normal(jax.random.fold_in(jax.random.key(seed), 1), (16, 512, 128), dtype=_x0.dtype)
    del _x0
    return _d

def reference(L0_attn_x, L0_attn_W, L0_ffn_gate_w, L0_ffn_w_gate_up, L0_ffn_w_down, L0_ffn_shared_w_gate_up, L0_ffn_shared_w_down, L1_attn_in_proj_w, L1_attn_conv_w, L1_attn_conv_b, L1_attn_x_proj_w, L1_attn_dt_proj_w, L1_attn_dt_proj_b, L1_attn_A_log, L1_attn_D, L1_attn_out_proj_w, L1_ffn_gate_w, L1_ffn_gate_b, L1_ffn_w1, L1_ffn_b1, L1_ffn_w3, L1_ffn_b3, L1_ffn_w2, L1_ffn_b2, L1_ffn_sw1, L1_ffn_sb1, L1_ffn_sw3, L1_ffn_sb3, L1_ffn_sw2, L1_ffn_sb2):

    def _L0_attn_ref(x, W):
        import jax, jax.numpy as jnp
        import numpy as np
        EPS = 1e-06
        D = x.shape[-1]
        qkv = x @ W
        q, k, v = jnp.split(qkv, 3, axis=-1)
        q = jax.nn.elu(q) + 1.0
        k = jax.nn.elu(k) + 1.0
        KV = jnp.einsum('bld,blh->bhd', k, v)
        k_sum = k.sum(axis=1)
        Z = 1.0 / (jnp.einsum('bld,bd->bl', q, k_sum) + EPS)
        V = jnp.einsum('bld,bhd,bl->blh', q, KV, Z)
        return V

    def _L0_ffn_ref(hidden_states, gate_w, w_gate_up, w_down, shared_w_gate_up, shared_w_down):
        import jax, jax.numpy as jnp
        import numpy as np
        E = 32
        K = 4
        H = 128
        I = 64
        B, S = (2, 256)
        T = B * S
        C = 128
        ROUTED_SCALE = 1.0

        def _silu_and_mul(gu):
            g, u = jnp.split(gu, 2, axis=-1)
            return jax.nn.silu(g) * u
        b, s, h = hidden_states.shape
        x = hidden_states.reshape(-1, h)
        t = x.shape[0]
        logits = x @ gate_w.T
        probs = jax.nn.softmax(logits, axis=-1)
        topk_w, topk_idx = jax.lax.top_k(probs, K)
        topk_w = topk_w / jnp.sum(topk_w, axis=-1, keepdims=True)
        topk_w = topk_w * ROUTED_SCALE
        e_flat = topk_idx.reshape(-1)
        w_flat = topk_w.reshape(-1)
        t_flat = jnp.repeat(jnp.arange(t), K)
        order = jnp.argsort(e_flat)
        e_s, w_s, t_s = (e_flat[order], w_flat[order], t_flat[order])
        counts = jax.ops.segment_sum(jnp.ones_like(e_s), e_s, num_segments=E)
        starts = jnp.cumsum(counts) - counts
        pos = jnp.arange(t * K) - starts[e_s]
        slot = jnp.minimum(pos, C)
        buf = jnp.zeros((E, C + 1, h), x.dtype).at[e_s, slot].set(x[t_s])
        gu = jnp.einsum('ech,ehi->eci', buf[:, :C], w_gate_up)
        expert_out = jnp.einsum('eci,eih->ech', _silu_and_mul(gu), w_down)
        expert_out = jnp.pad(expert_out, ((0, 0), (0, 1), (0, 0)))
        gate = jnp.where(pos < C, w_s, 0.0)[:, None]
        routed = jnp.zeros_like(x).at[t_s].add(expert_out[e_s, slot] * gate)
        shared = _silu_and_mul(x @ shared_w_gate_up) @ shared_w_down
        return (routed + shared).reshape(b, s, h)

    def _L1_attn_ref(x, in_proj_w, conv_w, conv_b, x_proj_w, dt_proj_w, dt_proj_b, A_log, D, out_proj_w):
        import jax, jax.numpy as jnp
        import numpy as np
        D_MODEL, D_STATE, D_CONV, EXPAND = (128, 16, 4, 2)
        D_INNER = EXPAND * D_MODEL
        BATCH, SEQ = (1, 512)

        def _selective_ssm(x, x_proj_w, dt_proj_w, dt_proj_b, A_log, D):
            xp = x @ x_proj_w.T
            dt_raw = xp[..., :1]
            B = xp[..., 1:D_STATE + 1]
            C = xp[..., D_STATE + 1:]
            dt = jax.nn.softplus(dt_raw @ dt_proj_w.T + dt_proj_b)
            A = -jnp.exp(A_log)
            dA = jnp.exp(jnp.einsum('bld,dn->bldn', dt, A))
            dBx = (dt * x)[..., None] * B[:, :, None, :]

            def step(h, inp):
                dA_t, dBx_t, C_t = inp
                h = dA_t * h + dBx_t
                y = jnp.einsum('bdn,bn->bd', h, C_t)
                return (h, y)
            h0 = jnp.zeros((x.shape[0], D_INNER, D_STATE), x.dtype)
            _, ys = jax.lax.scan(step, h0, (dA.transpose(1, 0, 2, 3), dBx.transpose(1, 0, 2, 3), C.transpose(1, 0, 2)))
            y = ys.transpose(1, 0, 2)
            return y + x * D
        xz = x @ in_proj_w.T
        xi, z = jnp.split(xz, 2, axis=-1)
        xc = jax.lax.conv_general_dilated(xi.transpose(0, 2, 1), conv_w, window_strides=(1,), padding=[(D_CONV - 1, 0)], feature_group_count=D_INNER, dimension_numbers=('NCH', 'OIH', 'NCH'))
        xc = (xc + conv_b[None, :, None]).transpose(0, 2, 1)
        xc = jax.nn.silu(xc)
        y = _selective_ssm(xc, x_proj_w, dt_proj_w, dt_proj_b, A_log, D)
        y = y * jax.nn.silu(z)
        return y @ out_proj_w.T

    def _L1_ffn_ref(x, gate_w, gate_b, w1, b1, w3, b3, w2, b2, sw1, sb1, sw3, sb3, sw2, sb2):
        import jax, jax.numpy as jnp
        import numpy as np
        from jax import lax
        D = 128
        H = 176
        E = 8
        K = 2
        ROUTER_SCALE = 1.0

        def _expert(x, w1, b1, w3, b3, w2, b2):
            h = jax.nn.silu((x @ w1 + b1) * (x @ w3 + b3))
            return h @ w2 + b2
        shape = x.shape
        xf = x.reshape(-1, D)
        T = xf.shape[0]
        scores = jax.nn.softmax(xf @ gate_w.T, axis=-1)
        biased = scores + gate_b
        _, idx = lax.top_k(biased, K)
        w = jnp.take_along_axis(scores, idx, axis=-1) * ROUTER_SCALE
        rw = jnp.zeros((T, E), dtype=xf.dtype).at[jnp.arange(T)[:, None], idx].add(w)
        h = jax.nn.silu((jnp.einsum('td,edh->teh', xf, w1) + b1) * (jnp.einsum('td,edh->teh', xf, w3) + b3))
        oe = jnp.einsum('teh,ehd->ted', h, w2) + b2
        y = jnp.einsum('te,ted->td', rw, oe)
        z = _expert(xf, sw1, sb1, sw3, sb3, sw2, sb2)
        return (y + z).reshape(shape)
    x = L0_attn_x
    x = _layernorm(x + _L0_attn_ref(x, L0_attn_W), axis=-1)
    x = _layernorm(x + _L0_ffn_ref(x, L0_ffn_gate_w, L0_ffn_w_gate_up, L0_ffn_w_down, L0_ffn_shared_w_gate_up, L0_ffn_shared_w_down), axis=-1)
    x = _layernorm(x + _L1_attn_ref(x, L1_attn_in_proj_w, L1_attn_conv_w, L1_attn_conv_b, L1_attn_x_proj_w, L1_attn_dt_proj_w, L1_attn_dt_proj_b, L1_attn_A_log, L1_attn_D, L1_attn_out_proj_w), axis=-1)
    x = _layernorm(x + _L1_ffn_ref(x, L1_ffn_gate_w, L1_ffn_gate_b, L1_ffn_w1, L1_ffn_b1, L1_ffn_w3, L1_ffn_b3, L1_ffn_w2, L1_ffn_b2, L1_ffn_sw1, L1_ffn_sb1, L1_ffn_sw3, L1_ffn_sb3, L1_ffn_sw2, L1_ffn_sb2), axis=-1)
    return x

_drawn_inputs = setup_inputs


def setup_inputs(seed=0):
    import zlib

    import numpy as np

    out = dict(_drawn_inputs(seed))
    spreads = {'L1_attn_conv_b': (0.0, 0.1), 'L1_attn_D': (1.0, 0.2)}
    factors = {'L0_attn_W': 4.126,
     'L0_ffn_gate_w': 8.0,
     'L0_ffn_w_gate_up': 8.0,
     'L0_ffn_w_down': 8.0,
     'L0_ffn_shared_w_gate_up': 8.0,
     'L0_ffn_shared_w_down': 8.0,
     'L1_ffn_gate_w': 8.0,
     'L1_ffn_gate_b': 8.0,
     'L1_ffn_w1': 8.0,
     'L1_ffn_b1': 8.0,
     'L1_ffn_w3': 8.0,
     'L1_ffn_b3': 8.0,
     'L1_ffn_w2': 8.0,
     'L1_ffn_b2': 28.448,
     'L1_ffn_sw1': 8.0,
     'L1_ffn_sb1': 8.0,
     'L1_ffn_sw3': 8.0,
     'L1_ffn_sb3': 8.0,
     'L1_ffn_sw2': 8.0,
     'L1_ffn_sb2': 15.786}
    for name, (base, spread) in spreads.items():
        noise = np.random.default_rng([zlib.crc32(name.encode()), seed]).standard_normal(out[name].shape)
        drawn = base * np.exp(spread * noise) if base else spread * noise
        out[name] = jnp.asarray(drawn.astype(out[name].dtype))
    for name, factor in factors.items():
        out[name] = (out[name] * factor).astype(out[name].dtype)
    return out
```

```python
from contextlib import ExitStack

import concourse.bass as bass
from concourse import mybir

F32 = mybir.dt.float32
BF16 = mybir.dt.bfloat16
U32 = mybir.dt.uint32
ALU = mybir.AluOpType
ACT = mybir.ActivationFunctionType
AX = mybir.AxisListType

P = 128
NB, SEQ, D = 16, 512, 128
TOK = NB * SEQ
TT = SEQ // P
E0, TOPK, CAP, I0 = 32, 4, 128, 64
XGW = D + E0
NSEG = 4
N_CONST = 12 + NSEG
SEG = TOK // NSEG
DI, NH, NS = 256, 2, 16
E1, H1 = 8, 176
SH_CH = 2
RT_CH = E1 * H1 // P
NCH = SH_CH + RT_CH
LN_EPS = 1e-5
Z_EPS = 1e-6
EG = 4


class Seq:

    def __init__(self, j, off):
        self.j, self.off, self.par = j, off, off % 2

    def at(self, per, k=0):
        return self.j * (2 * per) + (self.off * per + k)

    def half(self, per, k=0):
        return self.j * per + (self.off // 2 * per + k)


def need(eng, sem, value):
    if isinstance(value, int) and value <= 0:
        return
    eng.wait_ge(sem, value)


def schedule(eng, iteration):
    q = lambda b: Seq(0, b) if 0 <= b < NB else None
    for i in range(-1, 2):
        iteration(q(i + 1), q(i), q(i - 1), None)
    with eng.Fori(0, NB // 2 - 2) as j:
        for i in (2, 3):
            iteration(Seq(j, i + 1), Seq(j, i), Seq(j, i - 1), Seq(j, i - 2))
    for i in range(NB - 2, NB + 2):
        iteration(q(i + 1), q(i), q(i - 1), q(i - 2))


def build(nc, t, out):
    ctx = ExitStack()
    with ctx:
        def sb(name, shape, dt=F32):
            return ctx.enter_context(nc.sbuf_tensor(name, shape, dt))

        def sem(name):
            return ctx.enter_context(nc.semaphore(name))

        xg_d = nc.dram_tensor("xg_rows", (TOK + P, XGW), F32).ap()
        r_d = nc.dram_tensor("resid_rows", (TOK + P, D), F32).ap()
        mask_d = nc.dram_tensor("mask_by_expert", (E0, TOK), F32).ap()
        cand_d = nc.dram_tensor("candidates", (NSEG, E0, P), F32).ap()

        bank01 = ctx.enter_context(nc.psum_tensor("bank01", [P, 2, 512], F32))
        bank = {n: ctx.enter_context(nc.psum_tensor(f"bank{n}", [P, 512], F32)) for n in range(2, 8)}

        ident = sb("ident", [P, P])
        sel_bc = sb("sel_bc", [96, 2 * NS, P], BF16)
        sel_rw = sb("sel_rw", [E1 + 1, RT_CH, P])
        iota_e = sb("iota_e", [P, E0])
        neghalf = sb("neghalf", [P, TT])
        slot_no = sb("slot_no", [E0, P])

        wt = {n: sb("w_" + n, list(t[n].shape)) for n in (
            "Wq", "Wkv", "gw0", "sgu", "sd", "inp", "convw", "convb", "xpw", "dtrow", "dtw", "dtb",
            "alog", "dskip", "outp", "gw1", "gb1", "w1", "w3", "b1", "b3", "w2", "b2x")}

        aneg = sb("aneg", [P, NH, NS])

        with ExitStack() as early:
            def eb(name, shape, dt=F32):
                return early.enter_context(nc.sbuf_tensor(name, shape, dt))

            wgu, wd = eb("w_wgu", list(t["wgu"].shape)), eb("w_wd", list(t["wd"].shape))
            xt = [eb(f"xt{p}", [P, TT, D]) for p in range(2)]
            xT = [eb(f"xT{p}", [P, SEQ]) for p in range(2)]
            ek = eb("ek", [P, TT, D])
            rk = eb("rk", [P, TT, D])
            kf = eb("kf", [P, TT, D])
            eq = eb("eq", [P, SEQ])
            rq = eb("rq", [P, SEQ])
            qf = eb("qf", [P, SEQ])
            vext = eb("vext", [P, TT, D + 1])
            kvx = eb("kvx", [P, D + 1])
            den = eb("den", [P, TT])
            rz = eb("rz", [P, TT])
            pre = eb("pre", [P, TT, D])
            xg = [eb(f"xg{p}", [P, TT, XGW]) for p in range(2)]
            x1T = eb("x1T", [P, SEQ])
            tg = eb("tg", [I0, SEQ])
            sg = eb("sg", [I0, SEQ])
            hsh = eb("hsh", [I0, SEQ])
            lg = eb("lg", [P, TT, E0])
            top = eb("top", [P, TT, 8])
            topi = eb("topi", [P, TT, 8], U32)
            lsub = eb("lsub", [P, TT, E0])
            lexp = eb("lexp", [P, TT, E0])
            hot = eb("hot", [P, TT, TOPK, E0])
            mask = eb("mask", [P, TT, E0])
            gm = eb("gm", [P, TT, E0])
            gs = eb("gs", [P, TT])
            gr = eb("gr", [P, TT])
            resid = eb("resid", [P, TT, D])
            maskT = eb("maskT", [E0, SEQ])
            zero = eb("zero", [P, XGW])
            stats = eb("stats", [P, TT, 6])
            mv = eb("mv", [P, TT, 2])
            ve = eb("ve", [P, TT])
            rstd = eb("rstd", [P, TT])

            rev = eb("rev", [P, SEG])
            val = eb("val", [P, SEG])
            cand = eb("cand", [P, P])
            cval = eb("cval", [E0, NSEG * P])
            first = eb("first", [E0, P])
            empty = eb("empty", [E0, P])
            idxf = eb("idxf", [E0, P])
            idx = eb("idx", [P, E0], U32)

            xe = [eb(f"xe{p}", [P, EG, XGW]) for p in range(2)]
            ixg = [eb(f"ixg{p}", [P, EG], U32) for p in range(2)]
            ixs = [eb(f"ixs{p}", [P, EG], U32) for p in range(2)]
            xeT = eb("xeT", [P, EG, P])
            te = eb("te", [P, EG, I0])
            se = eb("se", [P, EG, I0])
            ae = eb("ae", [P, EG, I0])
            aeT = eb("aeT", [I0, EG, P])
            ge = eb("ge", [P, EG])
            ye = [eb(f"ye{p}", [P, EG, D]) for p in range(2)]


        rin = sb("rin", [P, TT, D])
        x2 = [sb(f"x2_{p}", [P, TT, D]) for p in range(2)]
        x2T = sb("x2T", [P, SEQ])
        xib = sb("xib", [P, NH, SEQ + 3])
        cv = sb("cv", [P, NH, SEQ])
        tc = sb("tc", [P, NH, SEQ])
        xc = [sb(f"xc{p}", [P, NH, SEQ]) for p in range(2)]
        tz = sb("tz", [P, NH, SEQ])
        zc = sb("zc", [P, NH, SEQ])
        zs = [sb(f"zs{p}", [P, NH, SEQ]) for p in range(2)]
        parts = [sb(f"parts{p}", [96, SEQ], BF16) for p in range(2)]
        xpf = sb("xpf", [96, SEQ])
        rest1 = sb("rest1", [96, SEQ])
        mid = sb("mid", [96, SEQ], BF16)
        dtp = sb("dtp", [P, NH, SEQ])
        dta = sb("dta", [P, NH, SEQ])
        dt_ = [sb(f"dt{p}", [P, NH, SEQ]) for p in range(2)]
        u = [sb(f"u{p}", [P, NH, SEQ]) for p in range(2)]
        dA = [sb(f"dA{k}", [P, NH, SEQ]) for k in range(2)]
        dbx = sb("dbx", [P, NH, SEQ])
        hst = sb("hst", [P, NH, SEQ])
        prod = [sb(f"prod{k}", [P, NH, SEQ]) for k in range(2)]
        yd = sb("yd", [P, NH, SEQ])
        y2 = sb("y2", [P, NH, SEQ])
        x3p = sb("x3p", [P, TT, D])
        x3 = [sb(f"x3_{p}", [P, TT, D]) for p in range(2)]
        x3T = sb("x3T", [P, SEQ])
        l1 = sb("l1", [P, TT, E1])
        l1m = sb("l1m", [P, TT])
        l1s = sb("l1s", [P, TT, E1])
        l1e = sb("l1e", [P, TT, E1])
        l1z = sb("l1z", [P, TT])
        l1r = sb("l1r", [P, TT])
        sc1 = sb("sc1", [P, TT, E1])
        bi1 = sb("bi1", [P, TT, E1])
        tp1 = sb("tp1", [P, TT, 8])
        ti1 = sb("ti1", [P, TT, 8], U32)
        ho1 = sb("ho1", [P, TT, 2, E1])
        hm1 = sb("hm1", [P, TT, E1])
        rw = sb("rw", [P, TT, E1 + 1])
        rwT = [sb(f"rwT{p}", [E1 + 1, SEQ]) for p in range(2)]
        ha = sb("ha", [P, SEQ])
        hg = [sb(f"hg{k}", [P, SEQ]) for k in range(2)]
        ht = [sb(f"ht{k}", [P, SEQ]) for k in range(2)]
        hs = [sb(f"hs{k}", [P, SEQ]) for k in range(2)]
        hh = [sb(f"hh{k}", [P, SEQ]) for k in range(2)]
        of = sb("of", [P, TT, D])
        ofin = sb("ofin", [P, TT, D])
        st1 = sb("st1", [P, TT, 6])
        mv1 = sb("mv1", [P, TT, 2])
        ve1 = sb("ve1", [P, TT])
        rs1 = sb("rs1", [P, TT])
        st2 = sb("st2", [P, TT, 6])
        mv2 = sb("mv2", [P, TT, 2])
        ve2 = sb("ve2", [P, TT])
        rs2 = sb("rs2", [P, TT])
        st3 = sb("st3", [P, TT, 6])
        mv3 = sb("mv3", [P, TT, 2])
        ve3 = sb("ve3", [P, TT])
        rs3 = sb("rs3", [P, TT])

        w_loaded, const_rdy, half_rdy, a_exp, zeros_stored = sem("w_loaded"), sem("const_rdy"), sem("half_rdy"), sem("a_exp"), sem("zeros_stored")
        dve_init = sem("dve_init")
        ldx0, ldx1, kv_mm, q_mm, ek_rdy = sem("ldx0"), sem("ldx1"), sem("kv_mm"), sem("q_mm"), sem("ek_rdy")
        v_rdy, rk_rdy, kf_rdy, eq_rdy, rq_rdy = sem("v_rdy"), sem("rk_rdy"), sem("kf_rdy"), sem("eq_rdy"), sem("rq_rdy")
        qf_rdy = sem("qf_rdy")
        kva_mm, kvx_rdy, o_mm, den_rdy, rz_rdy = sem("kva_mm"), sem("kvx_rdy"), sem("o_mm"), sem("den_rdy"), sem("rz_rdy")
        pre_rdy, ve_rdy, rstd_rdy = sem("pre_rdy"), sem("ve_rdy"), sem("rstd_rdy")
        x1_rdy = sem("x1_rdy")
        t_mm, x1T_rdy, gu_mm, l_mm, lg_rdy = sem("t_mm"), sem("x1T_rdy"), sem("gu_mm"), sem("l_mm"), sem("lg_rdy")
        tg_rdy, sg_rdy, hsh_rdy = sem("tg_rdy"), sem("sg_rdy"), sem("hsh_rdy")
        lexp_rdy = sem("lexp_rdy")
        d_mm, mt_mm = sem("d_mm"), sem("mt_mm")
        maskT_rdy, resid_rdy, st_xg0, st_xg1, st_r = sem("maskT_rdy"), sem("resid_rdy"), sem("st_xg0"), sem("st_xg1"), sem("st_r")
        st_m = sem("st_m")
        seg_loaded, val_rdy, cand_rdy, cand_stored, cand_loaded = sem("seg_loaded"), sem("val_rdy"), sem("cand_rdy"), sem("cand_stored"), sem("cand_loaded")
        first_rdy, empty_rdy, idxf_rdy, idx_mm, idx_rdy = sem("first_rdy"), sem("empty_rdy"), sem("idxf_rdy"), sem("idx_mm"), sem("idx_rdy")
        xe_got0, xe_got1, xeT_mm, xeT_rdy, gu_e = sem("xe_got0"), sem("xe_got1"), sem("xeT_mm"), sem("xeT_rdy"), sem("gu_e")
        te_rdy, se_rdy, ae_rdy, aeT_mm, aeT_rdy = sem("te_rdy"), sem("se_rdy"), sem("ae_rdy"), sem("aeT_mm"), sem("aeT_rdy")
        dn_mm, ge_rdy, ye_rdy, added = sem("dn_mm"), sem("ge_rdy"), sem("ye_rdy"), sem("added")
        ld_r, f_ve, f_rs = sem("ld_r"), sem("f_ve"), sem("f_rs")
        x2_rdy, x2T_mm, x2T_rdy, xi_mm, xib_rdy = sem("x2_rdy"), sem("x2T_mm"), sem("x2T_rdy"), sem("xi_mm"), sem("xib_rdy")
        cv_rdy = sem("cv_rdy")
        tc_rdy, xc_rdy, z_mm, tz_rdy, zs_rdy = sem("tc_rdy"), sem("xc_rdy"), sem("z_mm"), sem("tz_rdy"), sem("zs_rdy")
        xp_mm, parts1, rest_rdy, parts2, mid_rdy = sem("xp_mm"), sem("parts1"), sem("rest_rdy"), sem("parts2"), sem("mid_rdy")
        parts_rdy = sem("parts_rdy")
        dtr_mm, dtp_rdy, dta_rdy, dte_rdy, dtl_rdy = sem("dtr_mm"), sem("dtp_rdy"), sem("dta_rdy"), sem("dte_rdy"), sem("dtl_rdy")
        dt_rdy, u_rdy = sem("dt_rdy"), sem("u_rdy")
        bb_rdy, cb_rdy, da_rdy, dbx_rdy, scan_rdy = sem("bb_rdy"), sem("cb_rdy"), sem("da_rdy"), sem("dbx_rdy"), sem("scan_rdy")
        prod_rdy, y_mm = sem("prod_rdy"), sem("y_mm")
        yd_rdy, y2_rdy, op_mm, x3p_rdy = sem("yd_rdy"), sem("y2_rdy"), sem("op_mm"), sem("x3p_rdy")
        m_ve, m_rs, x3_rdy, x3T_mm = sem("m_ve"), sem("m_rs"), sem("x3_rdy"), sem("x3T_mm")
        x3T_rdy, l1_mm, l1_rdy = sem("x3T_rdy"), sem("l1_mm"), sem("l1_rdy")
        l1e_rdy = sem("l1e_rdy")
        rw_rdy = sem("rw_rdy")
        rwT_mm, rwT_rdy, h1_mm, h3_mm, ha_rdy = sem("rwT_mm"), sem("rwT_rdy"), sem("h1_mm"), sem("h3_mm"), sem("ha_rdy")
        hg_rdy, ht_rdy, hs_rdy, rwb_mm, hh_rdy = sem("hg_rdy"), sem("ht_rdy"), sem("hs_rdy"), sem("rwb_mm"), sem("hh_rdy")
        dn_done = sem("dn_done")
        of_rdy, o_ve, o_rs = sem("of_rdy"), sem("o_ve"), sem("o_rs")
        ofin_rdy, st_o = sem("ofin_rdy"), sem("st_o")
        zc_rdy, xpf_rdy, ixg_rdy, ixs_rdy = sem("zc_rdy"), sem("xpf_rdy"), sem("ixg_rdy"), sem("ixs_rdy")

        settled, b2_mm, taken, idxd_rdy, a_neg = sem("settled"), sem("b2_mm"), sem("taken"), sem("idxd_rdy"), sem("a_neg")
        route0, route1 = sem("route0"), sem("route1")

        ldx, st_xg, xe_got = [ldx0, ldx1], [st_xg0, st_xg1], [xe_got0, xe_got1]

        def settle(eng):
            eng.sem_inc(settled, 1)

        block = ctx.enter_context(nc.Block())

        kv_ps = bank01[:, :, :].rearrange("p a (b c) -> p (a b) c", b=2)
        o_ps = kv_ps
        q_ps, kva_ps, t_ps = bank[2], bank[3], bank[4]
        g_ps, u_ps, d_ps = bank[5], bank[6], bank[7]
        y_ps = bank01
        bb_ps, cb_ps, h1_ps, h3_ps, fo_ps, px_ps = bank[2], bank[3], bank[4], bank[5], bank[6], bank[7]
        blk4 = lambda a: a[:, :].rearrange("p (t c) -> p t c", t=TT)
        sel_e = lambda c: sel_rw[:, c - SH_CH, :]
        rows_of = lambda c: H1 - P if c == 1 else P
        N1 = NB * TT

        @block.sync
        def _(sp):
            for n, w in wt.items():
                sp.dma_start(w[:], t[n]).then_inc(w_loaded, 16)
            sp.dma_start(wgu[:], t["wgu"]).then_inc(w_loaded, 16)
            sp.dma_start(wd[:], t["wd"]).then_inc(w_loaded, 16)

            def load_x(s):
                for read, count in ((pre_rdy, s.at(TT, -TT)), (q_mm, s.at(1, -1))):
                    need(sp, read, count)
                    settle(sp)
                sp.dma_start(xt[s.par][:, :, :], t["x"][bass.ds(s.at(SEQ), SEQ), :].rearrange("(t p) d -> p t d", p=P)
                             ).then_inc(ldx[s.par], 16)
                sp.dma_start(xT[s.par][:, :], t["xT"][:, bass.ds(s.at(SEQ), SEQ)]).then_inc(ldx[s.par], 16)

            def store_routed(s):
                sp.wait_ge(resid_rdy, s.at(1, 1))
                sp.dma_start(r_d[bass.ds(s.at(SEQ), SEQ), :].rearrange("(t p) d -> p t d", p=P), resid[:, :, :]
                             ).then_inc(st_r, 16)
                sp.wait_ge(maskT_rdy, s.at(1, 1))
                settle(sp)
                sp.dma_start(mask_d[:, bass.ds(s.at(SEQ), SEQ)], maskT[:, :]).then_inc(st_m, 16)
                sp.wait_ge(route0, s.at(15, 15))
                sp.dma_start(xg_d[bass.ds(s.at(SEQ), SEQ), :].rearrange("(t p) d -> p t d", p=P), xg[s.par][:, :, :]
                             ).then_inc(st_xg[s.par], 16)

            load_x(Seq(0, 0))
            sp.wait_ge(dve_init, 1)
            sp.dma_start(xg_d[TOK:TOK + P, :], zero[:, :]).then_inc(zeros_stored, 16)
            sp.dma_start(r_d[TOK:TOK + P, :], zero[:, 0:D]).then_inc(zeros_stored, 16)
            load_x(Seq(0, 1))
            with sp.Fori(0, NB // 2 - 1) as j:
                for i in (1, 2):
                    load_x(Seq(j, i + 1))
                    store_routed(Seq(j, i - 1))
            store_routed(Seq(0, NB - 2))
            store_routed(Seq(0, NB - 1))

            sp.wait_ge(st_m, NB * 16)
            for k in range(NSEG):
                sp.dma_start(val[k * E0:(k + 1) * E0, :], mask_d[:, k * SEG:(k + 1) * SEG]).then_inc(seg_loaded, 16)
            sp.wait_ge(cand_rdy, CAP // 8)
            sp.dma_start(cand_d.rearrange("s e c -> (s e) c"), cand[:, :]).then_inc(cand_stored, 16)
            sp.wait_ge(cand_stored, 16)
            sp.dma_start(cval[:, :].rearrange("e (s c) -> e s c", s=NSEG), cand_d.rearrange("s e c -> e s c")
                         ).then_inc(cand_loaded, 16)

            def load_r(s):
                need(sp, x2_rdy, s.at(TT))
                sp.dma_start(rin[:, :, :], r_d[bass.ds(s.at(SEQ), SEQ), :].rearrange("(t p) d -> p t d", p=P)
                             ).then_inc(ld_r, 16)

            def store_out(s):
                sp.wait_ge(ofin_rdy, s.at(TT, TT))
                sp.dma_start(out[bass.ds(s.at(SEQ), SEQ), :].rearrange("(t p) d -> p t d", p=P), ofin[:, :, :]
                             ).then_inc(st_o, 16)

            sp.wait_ge(added, E0 * 16)
            load_r(Seq(0, 0))
            load_r(Seq(0, 1))
            load_r(Seq(0, 2))
            with sp.Fori(0, NB // 2 - 2) as j:
                for i in (2, 3):
                    load_r(Seq(j, i + 1))
                    store_out(Seq(j, i - 2))
            load_r(Seq(0, NB - 1))
            for b in range(NB - 4, NB):
                store_out(Seq(0, b))
            sp.wait_ge(st_o, NB * 16)

        @block.gpsimd
        def _(gp):
            made = [0]

            def make(ins):
                made[0] += 1
                ins.then_inc(const_rdy, 1)
                gp.wait_ge(const_rdy, made[0])

            make(gp.memset(ident[:, :], 0.0))
            make(gp.affine_select(out=ident[:, :], in_=ident[:, :], compare_op=ALU.not_equal, fill=1.0, base=0,
                                  pattern=[[-1, P]], channel_multiplier=1))
            make(gp.memset(neghalf[:, :], -0.5))
            make(gp.iota(iota_e[:, :], [[1, E0]], base=0, channel_multiplier=0, allow_small_or_imprecise_dtypes=True))
            make(gp.iota(slot_no[:, :], [[1, P]], base=0, channel_multiplier=0, allow_small_or_imprecise_dtypes=True))
            for k in range(NSEG):
                make(gp.iota(rev[k * E0:(k + 1) * E0, :], [[-1, SEG]], base=TOK - k * SEG, channel_multiplier=0,
                             allow_small_or_imprecise_dtypes=True))
            make(gp.memset(sel_rw[:, :, :], 1.0))
            make(gp.affine_select(out=sel_rw[:, :, :], in_=sel_rw[:, :, :], compare_op=ALU.is_ge, fill=0.0, base=0,
                                  pattern=[[P, RT_CH], [1, P]], channel_multiplier=-H1))
            make(gp.affine_select(out=sel_rw[:, :, :], in_=sel_rw[:, :, :], compare_op=ALU.is_ge, fill=0.0, base=H1 - 1,
                                  pattern=[[-P, RT_CH], [-1, P]], channel_multiplier=H1))
            make(gp.memset(sel_bc[:, :, :], 0.0))
            for part in range(3):
                make(gp.affine_select(out=sel_bc[:, :, :], in_=sel_bc[:, :, :], compare_op=ALU.not_equal, fill=1.0,
                                      base=-part * 2 * NS, pattern=[[-1, 2 * NS], [0, P]], channel_multiplier=1))

            def rsqrt(dst, src, s, ready, done):
                gp.wait_ge(ready, s.at(9, 9))
                gp.tensor_tensor(dst[:, :], src[:, :], neghalf[:, :], ALU.pow).then_inc(done, 1)

            rsqrt(rstd, ve, Seq(0, 0), ve_rdy, rstd_rdy)
            with gp.Fori(0, NB // 2 - 1) as j:
                for i in (1, 2):
                    rsqrt(rstd, ve, Seq(j, i), ve_rdy, rstd_rdy)
            rsqrt(rstd, ve, Seq(0, NB - 1), ve_rdy, rstd_rdy)

            gp.wait_ge(idx_rdy, 1)
            for q in (0, 1):
                gp.wait_ge(st_xg[q], NB // 2 * 16)
            gp.wait_ge(st_r, NB * 16)
            gp.wait_ge(zeros_stored, 32)

            def gather(s):
                need(gp, ye_rdy, s.at(1, -1))
                for k in range(EG):
                    gp.tensor_copy(ixg[s.par][:, k:k + 1], idx[:, bass.ds(s.at(EG, k), 1)]).then_inc(ixg_rdy, 1)
                gp.wait_ge(ixg_rdy, s.at(EG, EG))
                settle(gp)
                for k in range(EG):
                    gp.indirect_dma_start(xe[s.par][:, k, :], None, xg_d[:, :], bass.IndirectOffsetOnAxis(ixg[s.par][:, k:k + 1], 0)
                                          ).then_inc(xe_got[s.par], 16)

            def scatter(s):
                gp.wait_ge(ye_rdy, s.at(1, 1))
                for k in range(EG):
                    gp.tensor_copy(ixs[s.par][:, k:k + 1], idx[:, bass.ds(s.at(EG, k), 1)]).then_inc(ixs_rdy, 1)
                gp.wait_ge(ixs_rdy, s.at(EG, EG))
                for k in range(EG):
                    need(gp, added, s.at(EG * 16, k * 16))
                    settle(gp)
                    gp.indirect_dma_start(r_d[:, :], bass.IndirectOffsetOnAxis(ixs[s.par][:, k:k + 1], 0), ye[s.par][:, k, :], None,
                                          compute_op=ALU.add).then_inc(added, 16)

            gather(Seq(0, 0))
            gather(Seq(0, 1))
            with gp.Fori(0, E0 // EG // 2 - 1) as j:
                for i in (0, 1):
                    scatter(Seq(j, i))
                    gather(Seq(j, i + 2))
            scatter(Seq(0, E0 // EG - 2))
            scatter(Seq(0, E0 // EG - 1))

            def front(s, n):
                if n == 3:
                    rsqrt(rs1, ve1, s, f_ve, f_rs)
                if n == 15:
                    gp.wait_ge(dt_rdy, s.at(1, 1))
                    need(gp, dbx_rdy, s.at(NS, -NS))
                    gp.tensor_tensor(u[s.par][:, :, :], dt_[s.par][:, :, :], xc[s.par][:, :, :], ALU.mult).then_inc(u_rdy, 1)

            def experts(s, n):
                if n == 0:
                    gp.wait_ge(yd_rdy, s.at(NH, NH))
                    need(gp, op_mm, s.at(1))
                    gp.tensor_tensor(y2[:, :, :], yd[:, :, :], zs[s.par][:, :, :], ALU.mult).then_inc(y2_rdy, 1)
                if n == 2:
                    rsqrt(rs2, ve2, s, m_ve, m_rs)

            def tail(s, n):
                if n == 3:
                    rsqrt(rs3, ve3, s, o_ve, o_rs)

            def iteration(f, s, m, o):
                for n in range(NS):
                    if m:
                        experts(m, n)
                    if o:
                        tail(o, n)
                    if f:
                        front(f, n)

            gp.wait_ge(added, E0 * 16)
            schedule(gp, iteration)

        @block.scalar
        def _(act):
            act.wait_ge(w_loaded, 16 * (len(wt) + 2))
            act.activation(aneg[:, :, :], wt["alog"][:, :, :], ACT.Exp).then_inc(a_exp, 1)

            def stage1(a, r):
                if a:
                    act.wait_ge(kv_mm, a.at(1, 1))
                    need(act, kf_rdy, a.at(1))
                    act.activation(ek[:, :, :], kv_ps[:, :, 0:D], ACT.Exp).then_inc(ek_rdy, 1)
                    need(act, kva_mm, a.at(1))
                    act.activation(vext[:, :, 0:D], kv_ps[:, :, D:2 * D], ACT.Copy).then_inc(v_rdy, 1)
                    act.wait_ge(q_mm, a.at(1, 1))
                    need(act, qf_rdy, a.at(1))
                    act.activation(eq[:, :], q_ps[:, :], ACT.Exp).then_inc(eq_rdy, 1)
                if r:
                    act.wait_ge(t_mm, r.at(1, 1))
                    need(act, l_mm, r.at(1))
                    act.activation(x1T[:, :], t_ps[:, :], ACT.Copy).then_inc(x1T_rdy, 1)
                if a:
                    act.wait_ge(kva_mm, a.at(1, 1))
                    need(act, o_mm, a.at(1))
                    act.activation(kvx[:, :], kva_ps[:, 0:D + 1], ACT.Copy).then_inc(kvx_rdy, 1)
                if r:
                    act.wait_ge(l_mm, r.at(1, 1))
                    need(act, route0, r.at(15))
                    act.activation(lg[:, :, :], t_ps[:, 0:TT * E0].rearrange("p (t e) -> p t e", t=TT), ACT.Copy
                                   ).then_inc(lg_rdy, 1)
                    act.wait_ge(gu_mm, r.at(1, 1))
                    need(act, sg_rdy, r.at(1))
                    act.activation(tg[:, :], g_ps[0:I0, :], ACT.Tanh).then_inc(tg_rdy, 1)
                    act.wait_ge(route0, r.at(15, 5))
                    need(act, route0, r.at(15))
                    act.activation(lexp[:, :, :], lsub[:, :, :], ACT.Exp).then_inc(lexp_rdy, 1)
                    act.wait_ge(mt_mm, r.at(1, 1))
                    need(act, st_m, r.at(16))
                    act.activation(maskT[:, :], kva_ps[0:E0, :], ACT.Copy).then_inc(maskT_rdy, 1)

            stage1(Seq(0, 0), None)
            with act.Fori(0, NB // 2 - 1) as j:
                for i in (1, 2):
                    stage1(Seq(j, i), Seq(j, i - 1))
            stage1(Seq(0, NB - 1), Seq(0, NB - 2))
            stage1(None, Seq(0, NB - 1))

            def group(s):
                act.wait_ge(xeT_mm, s.at(1, 1))
                need(act, gu_e, s.at(1))
                act.activation(xeT[:, :, :], blk4(bank[2]), ACT.Copy).then_inc(xeT_rdy, 1)
                act.wait_ge(gu_e, s.at(1, 1))
                need(act, se_rdy, s.at(1))
                act.activation(te[:, :, :], blk4(bank[3])[:, :, 0:I0], ACT.Tanh, scale=0.5).then_inc(te_rdy, 1)
                act.wait_ge(aeT_mm, s.at(1, 1))
                need(act, dn_mm, s.at(1))
                act.activation(aeT[:, :, :], blk4(bank[4])[0:I0], ACT.Copy).then_inc(aeT_rdy, 1)

            with act.Fori(0, E0 // EG // 2) as j:
                for i in (0, 1):
                    group(Seq(j, i))

            def front(s, n):
                if n == 4:
                    act.wait_ge(x2T_mm, s.at(1, 1))
                    act.activation(x2T[:, :], px_ps[:, :], ACT.Copy).then_inc(x2T_rdy, 1)
                if n in (5, 6):
                    h = n - 5
                    act.wait_ge(xi_mm, s.at(NH, h + 1))
                    need(act, cv_rdy, s.at(8, 4 * h - 4))
                    act.activation(xib[:, h, 3:SEQ + 3], px_ps[:, :], ACT.Copy).then_inc(xib_rdy, 1)
                if n in (7, 8):
                    h = n - 7
                    act.wait_ge(z_mm, s.at(NH, h + 1))
                    need(act, zs_rdy, s.at(NH, h + 1 - NH))
                    act.activation(tz[:, h, :], px_ps[:, :], ACT.Tanh).then_inc(tz_rdy, 1)
                    act.activation(zc[:, h, :], px_ps[:, :], ACT.Copy).then_inc(zc_rdy, 1)
                if n in (8, 9):
                    h = n - 8
                    act.wait_ge(cv_rdy, s.at(8, 4 * h + 4))
                    need(act, xc_rdy, s.at(1))
                    act.activation(tc[:, h, :], cv[:, h, :], ACT.Tanh).then_inc(tc_rdy, 1)
                if n == 11:
                    act.wait_ge(xp_mm, s.at(1, 1))
                    need(act, cb_rdy, s.at(NS, -NS))
                    need(act, parts_rdy, s.at(1))
                    act.activation(parts[s.par][:, :], px_ps[0:96, :], ACT.Copy).then_inc(parts1, 1)
                    act.activation(xpf[:, :], px_ps[0:96, :], ACT.Copy).then_inc(xpf_rdy, 1)
                if n == 12:
                    act.wait_ge(dtr_mm, s.at(1, 1))
                    need(act, dt_rdy, s.at(1))
                    for h in range(NH):
                        act.activation(dtp[:, h, :], px_ps[:, :], ACT.Identity, bias=wt["dtb"][:, h:h + 1],
                                       scale=wt["dtw"][:, h:h + 1]).then_inc(dtp_rdy, 1)
                if n == 13:
                    act.wait_ge(dtp_rdy, s.at(NH, NH))
                    act.activation(dta[:, :, :], dtp[:, :, :], ACT.Abs).then_inc(dta_rdy, 1)
                    act.wait_ge(dta_rdy, s.at(1, 1))
                    act.activation(dta[:, :, :], dta[:, :, :], ACT.Exp, scale=-1.0).then_inc(dte_rdy, 1)
                    act.wait_ge(dte_rdy, s.at(1, 1))
                    act.activation(dta[:, :, :], dta[:, :, :], ACT.Ln, bias=1.0).then_inc(dtl_rdy, 1)

            def scan_step(s, n):
                if n == 0:
                    act.wait_ge(dt_rdy, s.at(1, 1))
                need(act, scan_rdy, s.at(NS, n - 1))
                for h in range(NH):
                    act.activation(dA[n % 2][:, h, 1:SEQ], dt_[s.par][:, h, 1:SEQ], ACT.Exp, scale=aneg[:, h, n:n + 1]
                                   ).then_inc(da_rdy, 1)

            def chunk_a(s, c):
                act.wait_ge(h1_mm, s.at(NCH, c + 1))
                need(act, hg_rdy, s.at(NCH, c))
                k = rows_of(c)
                act.activation(ha[0:k, :], h1_ps[0:k, :], ACT.Identity, bias=wt["b1"][0:k, c:c + 1]).then_inc(ha_rdy, 1)

            def chunk_t(s, c):
                act.wait_ge(hg_rdy, s.at(NCH, c + 1))
                need(act, hs_rdy, s.at(NCH, c - 1))
                k = rows_of(c)
                act.activation(ht[c % 2][0:k, :], hg[c % 2][0:k, :], ACT.Tanh).then_inc(ht_rdy, 1)

            def experts_a(s, n):
                if n == 3:
                    act.wait_ge(x3T_mm, s.at(1, 1))
                    act.activation(x3T[:, :], h3_ps[:, :], ACT.Copy).then_inc(x3T_rdy, 1)
                if n == 4:
                    act.wait_ge(l1_mm, s.at(1, 1))
                    act.activation(l1[:, :, :], px_ps[:, 0:TT * E1].rearrange("p (t e) -> p t e", t=TT), ACT.Copy
                                   ).then_inc(l1_rdy, 1)
                if n == 5:
                    act.wait_ge(route1, s.at(16, 2))
                    act.activation(l1e[:, :, :], l1s[:, :, :], ACT.Exp).then_inc(l1e_rdy, 1)
                if n == 6:
                    act.wait_ge(rwT_mm, s.at(1, 1))
                    act.activation(rwT[s.par][:, :], px_ps[0:E1 + 1, :], ACT.Copy).then_inc(rwT_rdy, 1)

            def iteration(f, s, m, o):
                for n in range(NS):
                    if s:
                        scan_step(s, n)
                    if o and n == 0:
                        chunk_a(o, NCH - 1)
                    if m and n >= 4:
                        chunk_a(m, n - 4)
                    if f:
                        front(f, n)
                    if m:
                        experts_a(m, n)
                    if o and n == 0:
                        chunk_t(o, NCH - 1)
                    if m and n >= 4:
                        chunk_t(m, n - 4)

            act.wait_ge(added, E0 * 16)
            act.wait_ge(half_rdy, 6)
            act.wait_ge(a_neg, 1)
            schedule(act, iteration)

        @block.tensor
        def _(pe):
            mm = pe.matmul
            tile = lambda k: slice(k * P, (k + 1) * P)
            pe.wait_ge(w_loaded, 16 * (len(wt) + 2))
            pe.wait_ge(const_rdy, N_CONST)
            pe.wait_ge(half_rdy, 6)
            pe.wait_ge(dve_init, 2)

            def stage1(a, r):
                if a:
                    pe.wait_ge(ldx[a.par], a.half(32, 32))
                    need(pe, pre_rdy, a.at(TT))
                    for k in range(TT):
                        last = mm(kv_ps[:, k, :], xT[a.par][:, tile(k)], wt["Wkv"][:, :], start=True, stop=True)
                    last.then_inc(kv_mm, 1)
                    need(pe, eq_rdy, a.at(1))
                    need(pe, rq_rdy, a.at(1))
                    mm(q_ps[:, :], wt["Wq"][:, :], xT[a.par][:, :], start=True, stop=True).then_inc(q_mm, 1)
                if r:
                    pe.wait_ge(x1_rdy, r.at(TT, TT))
                    need(pe, lg_rdy, r.at(1))
                    for k in range(TT):
                        last = pe.transpose(t_ps[:, tile(k)], xg[r.par][:, k, 0:D], ident[:, :])
                    last.then_inc(t_mm, 1)
                if a:
                    pe.wait_ge(kf_rdy, a.at(1, 1))
                    pe.wait_ge(v_rdy, a.at(1, 1))
                    need(pe, maskT_rdy, a.at(1, -1))
                    for k in range(TT):
                        last = mm(kva_ps[:, 0:D + 1], kf[:, k, :], vext[:, k, :], start=(k == 0), stop=(k == TT - 1))
                    last.then_inc(kva_mm, 1)
                if r:
                    pe.wait_ge(x1T_rdy, r.at(1, 1))
                    need(pe, hsh_rdy, r.at(1))
                    mm(g_ps[0:I0, :], wt["sgu"][:, 0:I0], x1T[:, :], start=True, stop=True)
                    mm(u_ps[0:I0, :], wt["sgu"][:, I0:2 * I0], x1T[:, :], start=True, stop=True).then_inc(gu_mm, 1)
                    for k in range(TT):
                        last = mm(t_ps[:, k * E0:(k + 1) * E0], x1T[:, tile(k)], wt["gw0"][:, :], start=True, stop=True)
                    last.then_inc(l_mm, 1)
                if a:
                    pe.wait_ge(kvx_rdy, a.at(1, 1))
                    pe.wait_ge(qf_rdy, a.at(1, 1))
                    for k in range(TT):
                        last = mm(o_ps[:, k, 0:D + 1], qf[:, tile(k)], kvx[:, :], start=True, stop=True)
                    last.then_inc(o_mm, 1)
                if r:
                    pe.wait_ge(hsh_rdy, r.at(1, 1))
                    need(pe, resid_rdy, r.at(1))
                    for k in range(TT):
                        last = mm(d_ps[:, tile(k)], hsh[:, tile(k)], wt["sd"][:, :], start=True, stop=True)
                    last.then_inc(d_mm, 1)
                    pe.wait_ge(route0, r.at(15, 11))
                    pe.wait_ge(kvx_rdy, a.at(1, 1) if a else NB)
                    for k in range(TT):
                        last = pe.transpose(kva_ps[0:E0, tile(k)], mask[:, k, :], ident[:, :])
                    last.then_inc(mt_mm, 1)

            stage1(Seq(0, 0), None)
            with pe.Fori(0, NB // 2 - 1) as j:
                for i in (1, 2):
                    stage1(Seq(j, i), Seq(j, i - 1))
            stage1(Seq(0, NB - 1), Seq(0, NB - 2))
            stage1(None, Seq(0, NB - 1))

            pe.wait_ge(idxf_rdy, 1)
            pe.transpose(bank[6][:, 0:E0], idxf[:, :], ident[0:E0, 0:E0]).then_inc(idx_mm, 1)

            def group(s):
                pe.wait_ge(xe_got[s.par], s.half(16 * EG, 16 * EG))
                need(pe, xeT_rdy, s.at(1))
                for k in range(EG):
                    last = pe.transpose(bank[2][:, tile(k)], xe[s.par][:, k, 0:D], ident[:, :])
                last.then_inc(xeT_mm, 1)
                pe.wait_ge(xeT_rdy, s.at(1, 1))
                need(pe, ae_rdy, s.at(1))
                for k in range(EG):
                    last = mm(bank[3][:, tile(k)], xeT[:, k, :], wgu[:, bass.ds(s.at(EG, k), 1), :], start=True, stop=True)
                last.then_inc(gu_e, 1)
                pe.wait_ge(ae_rdy, s.at(1, 1))
                need(pe, aeT_rdy, s.at(1))
                settle(pe)
                for k in range(EG):
                    last = pe.transpose(bank[4][0:I0, tile(k)], ae[:, k, :], ident[:, :])
                last.then_inc(aeT_mm, 1)
                pe.wait_ge(aeT_rdy, s.at(1, 1))
                need(pe, ye_rdy, s.at(1))
                for k in range(EG):
                    last = mm(bank[5][:, tile(k)], aeT[:, k, :], wd[:, bass.ds(s.at(EG, k), 1), :], start=True, stop=True)
                last.then_inc(dn_mm, 1)

            with pe.Fori(0, E0 // EG // 2) as j:
                for i in (0, 1):
                    group(Seq(j, i))

            held = [None]

            def px_wait(sem_, value):
                if held[0]:
                    pe.wait_ge(*held[0])
                held[0] = (sem_, value)

            def front(s, n):
                if n == 4:
                    pe.wait_ge(x2_rdy, s.at(TT, TT))
                    px_wait(x2T_rdy, s.at(1, 1))
                    for k in range(TT):
                        last = pe.transpose(px_ps[:, tile(k)], x2[s.par][:, k, :], ident[:, :])
                    last.then_inc(x2T_mm, 1)
                if n in (5, 6):
                    pe.wait_ge(x2T_rdy, s.at(1, 1))
                    px_wait(xib_rdy, s.at(NH, n - 4))
                    mm(px_ps[:, :], wt["inp"][:, tile(n - 5)], x2T[:, :], start=True, stop=True).then_inc(xi_mm, 1)
                if n in (7, 8):
                    px_wait(zc_rdy, s.at(NH, n - 6))
                    mm(px_ps[:, :], wt["inp"][:, tile(n - 5)], x2T[:, :], start=True, stop=True).then_inc(z_mm, 1)
                if n in (11, 12):
                    pe.wait_ge(xc_rdy, s.at(1, 1))
                    w, done, read, per = (("xpw", xp_mm, xpf_rdy, 1), ("dtrow", dtr_mm, dtp_rdy, NH))[n - 11]
                    px_wait(read, s.at(per, per))
                    for h in range(NH):
                        last = mm(px_ps[:, :], wt[w][:, h, :], xc[s.par][:, h, :], start=(h == 0), stop=(h == NH - 1))
                    last.then_inc(done, 1)

            def spread_b(s, n):
                if n == 0:
                    pe.wait_ge(parts_rdy, s.at(1, 1))
                need(pe, dbx_rdy, s.at(NS, n))
                mm(bb_ps[:, :], sel_bc[:, n, :], parts[s.par][:, :], start=True, stop=True).then_inc(bb_rdy, 1)

            def spread_c(s, n):
                need(pe, prod_rdy, s.at(NS, n))
                mm(cb_ps[:, :], sel_bc[:, NS + n, :], parts[s.par][:, :], start=True, stop=True).then_inc(cb_rdy, 1)

            def add_state(s, n):
                if n == 0:
                    need(pe, yd_rdy, s.at(NH))
                pe.wait_ge(prod_rdy, s.at(NS, n + 1))
                for h in range(NH):
                    last = mm(y_ps[:, h, :], ident[:, :], prod[n % 2][:, h, :], start=(n == 0), stop=(n == NS - 1),
                              skip_group_check=True)
                last.then_inc(y_mm, 1)

            def hidden(s, c):
                if c == 0:
                    pe.wait_ge(x3T_rdy, s.at(1, 1))
                    pe.wait_ge(x3p_rdy, s.at(1, 1))
                pe.wait_ge(ha_rdy, s.at(NCH, c)) if c else None
                k = rows_of(c)
                mm(h1_ps[0:k, :], wt["w1"][:, c, 0:k], x3T[:, :], start=True, stop=True).then_inc(h1_mm, 1)
                pe.wait_ge(hg_rdy, s.at(NCH, c)) if c else None
                mm(h3_ps[0:k, :], wt["w3"][:, c, 0:k], x3T[:, :], start=True, stop=True).then_inc(h3_mm, 1)

            def spread_w(s, c):
                pe.wait_ge(rwT_rdy, s.at(1, 1))
                px_wait(hh_rdy, s.at(RT_CH, c - SH_CH + 1))
                mm(px_ps[:, :], sel_e(c), rwT[s.par][:, :], start=True, stop=True).then_inc(rwb_mm, 1)

            def down(s, c):
                k = rows_of(c)
                if c == 0:
                    need(pe, of_rdy, s.at(1))
                if c < SH_CH:
                    pe.wait_ge(hs_rdy, s.at(NCH, c + 1))
                else:
                    pe.wait_ge(hh_rdy, s.at(RT_CH, c - SH_CH + 1))
                h = (hs if c < SH_CH else hh)[c % 2]
                for q in range(TT):
                    last = mm(fo_ps[:, tile(q)], h[0:k, tile(q)], wt["w2"][0:k, c, :], start=(c == 0 and q == 0),
                              stop=False, skip_group_check=True)
                last.then_inc(dn_done, 1)

            def biases(s):
                for q in range(TT):
                    last = mm(fo_ps[:, tile(q)], rwT[s.par][:, tile(q)], wt["b2x"][:, :], start=False,
                              stop=True, skip_group_check=True)
                last.then_inc(b2_mm, 1)

            def experts(s, n):
                if n == 1:
                    pe.wait_ge(y2_rdy, s.at(1, 1))
                    need(pe, ha_rdy, s.at(NCH))
                    for k in range(TT):
                        for h in range(NH):
                            last = mm(h1_ps[:, tile(k)], y2[:, h, tile(k)], wt["outp"][:, h, :], start=(h == 0),
                                      stop=(h == NH - 1))
                    last.then_inc(op_mm, 1)
                if n == 3:
                    pe.wait_ge(x3_rdy, s.at(TT, TT))
                    need(pe, hg_rdy, s.at(NCH))
                    for k in range(TT):
                        last = pe.transpose(h3_ps[:, tile(k)], x3[s.par][:, k, :], ident[:, :])
                    last.then_inc(x3T_mm, 1)
                if n >= 4:
                    hidden(s, n - 4)

            def experts_x(s, n):
                if n == 4:
                    px_wait(l1_rdy, s.at(1, 1))
                    for k in range(TT):
                        last = mm(px_ps[:, k * E1:(k + 1) * E1], x3T[:, tile(k)], wt["gw1"][:, :], start=True, stop=True)
                    last.then_inc(l1_mm, 1)
                if n == 6:
                    pe.wait_ge(rw_rdy, s.at(1, 1))
                    px_wait(rwT_rdy, s.at(1, 1))
                    for k in range(TT):
                        last = pe.transpose(px_ps[0:E1 + 1, tile(k)], rw[:, k, :], ident[:, :])
                    last.then_inc(rwT_mm, 1)
                if n >= 5 + SH_CH:
                    spread_w(s, n - 5)
                if n >= 6:
                    down(s, n - 6)

            def tail(s, n):
                if n == 0:
                    hidden(s, NCH - 1)
                    spread_w(s, NCH - 2)
                    down(s, NCH - 3)
                if n == 1:
                    spread_w(s, NCH - 1)
                    down(s, NCH - 2)
                if n == 2:
                    down(s, NCH - 1)
                    biases(s)

            def iteration(f, s, m, o):
                if o:
                    held[0] = (hh_rdy, o.at(RT_CH, RT_CH - 2))
                for n in range(NS):
                    if s:
                        if n == 0:
                            spread_b(s, 0)
                        spread_c(s, n)
                        if n:
                            add_state(s, n - 1)
                        if n < NS - 1:
                            spread_b(s, n + 1)
                    if o:
                        tail(o, n)
                    if m:
                        experts(m, n)
                    if f:
                        front(f, n)
                    if m:
                        experts_x(m, n)
                if s:
                    add_state(s, NS - 1)

            pe.wait_ge(added, E0 * 16)
            schedule(pe, iteration)

        @block.vector
        def _(dve):
            tt, ts, stt = dve.tensor_tensor, dve.tensor_scalar, dve.scalar_tensor_tensor

            def spread(a, shape):
                return a.to_broadcast(shape)

            dve.memset(zero[:, :], 0.0).then_inc(dve_init, 1)
            dve.memset(vext[:, :, D:D + 1], 1.0).then_inc(dve_init, 1)
            dve.wait_ge(w_loaded, 16 * (len(wt) + 2))
            for w in (wt["sgu"][:, 0:I0], wt["inp"][:, DI:2 * DI], wt["convw"][:, :, :], wt["convb"][:, :],
                      wt["w1"][:, :, :], wt["b1"][:, :]):
                ts(w, w, 0.5, None, ALU.mult).then_inc(half_rdy, 1)
            dve.wait_ge(a_exp, 1)
            ts(aneg[:, :, :], aneg[:, :, :], -1.0, None, ALU.mult).then_inc(a_neg, 1)
            dve.wait_ge(const_rdy, N_CONST)

            def stats_of(src, st, m, v, s, done):
                for k in range(TT):
                    dve.bn_stats(st[:, k, :], src[:, k, :]).then_inc(done, 1)
                dve.wait_ge(done, s.at(9, 4))
                settle(dve)
                for k in range(TT):
                    dve.bn_aggr(m[:, k, :], st[:, k, :]).then_inc(done, 1)
                dve.wait_ge(done, s.at(9, 8))
                ts(v[:, :], m[:, :, 1], LN_EPS, None, ALU.add).then_inc(done, 1)

            def normalise(dst, src, m, r, s, ready, done):
                dve.wait_ge(ready, s.at(1, 1))
                for k in range(TT):
                    ts(dst[:, k, 0:D], src[:, k, :], m[:, k, 0:1], r[:, k:k + 1], ALU.subtract, ALU.mult).then_inc(done, 1)

            def one_hot(dst, index, k, width):
                a = iota_e[:, 0:width].rearrange("p (a b e) -> p a b e", a=1, b=1)
                b = index[:, :, 0:k].rearrange("p t (k e) -> p t k e", e=1)
                return tt(dst[:, :, :, :], a.to_broadcast([P, TT, k, width]), b.to_broadcast([P, TT, k, width]), ALU.is_equal)

            def col(a, width):
                return a[:, :].rearrange("p (t e) -> p t e", e=1).to_broadcast([P, TT, width])

            def stage1(a, r):
                if a:
                    dve.wait_ge(v_rdy, a.at(1, 1))
                    ts(rk[:, :, :], kv_ps[:, :, 0:D], 0.0, 1.0, ALU.max, ALU.add).then_inc(rk_rdy, 1)
                    dve.wait_ge(eq_rdy, a.at(1, 1))
                    ts(rq[:, :], q_ps[:, :], 0.0, 1.0, ALU.max, ALU.add).then_inc(rq_rdy, 1)
                    dve.wait_ge(rk_rdy, a.at(1, 1))
                    need(dve, kva_mm, a.at(1))
                    tt(kf[:, :, :], ek[:, :, :], rk[:, :, :], ALU.min).then_inc(kf_rdy, 1)
                    dve.wait_ge(rq_rdy, a.at(1, 1))
                    need(dve, o_mm, a.at(1))
                    tt(qf[:, :], eq[:, :], rq[:, :], ALU.min).then_inc(qf_rdy, 1)
                if r:
                    dve.wait_ge(lg_rdy, r.at(1, 1))
                    settle(dve)
                    for k in range(TT):
                        dve.max(top[:, k, :], lg[:, k, :]).then_inc(route0, 1)
                    dve.wait_ge(route0, r.at(15, 4))
                    tt(lsub[:, :, :], lg[:, :, :], top[:, :, 0:1].to_broadcast([P, TT, E0]), ALU.subtract).then_inc(route0, 1)
                    for k in range(TT):
                        dve.max_index(topi[:, k, :], top[:, k, :], lg[:, k, :]).then_inc(route0, 1)
                    dve.wait_ge(tg_rdy, r.at(1, 1))
                    stt(sg[:, :], tg[:, :], 1.0, g_ps[0:I0, :], ALU.add, ALU.mult).then_inc(sg_rdy, 1)
                    dve.wait_ge(route0, r.at(15, 9))
                    one_hot(hot, topi, TOPK, E0).then_inc(route0, 1)
                    dve.wait_ge(sg_rdy, r.at(1, 1))
                    need(dve, d_mm, r.at(1))
                    tt(hsh[:, :], sg[:, :], u_ps[0:I0, :], ALU.mult).then_inc(hsh_rdy, 1)
                    dve.wait_ge(route0, r.at(15, 10))
                    need(dve, mt_mm, r.at(1))
                    dve.tensor_reduce(mask[:, :, :], hot[:, :, :, :].rearrange("p t k e -> p t e k"), AX.X, ALU.add
                                      ).then_inc(route0, 1)
                if a:
                    dve.wait_ge(o_mm, a.at(1, 1))
                    ts(den[:, :], o_ps[:, :, D], Z_EPS, None, ALU.add).then_inc(den_rdy, 1)
                    dve.wait_ge(den_rdy, a.at(1, 1))
                    dve.reciprocal(rz[:, :], den[:, :]).then_inc(rz_rdy, 1)
                if r:
                    dve.wait_ge(route0, r.at(15, 11))
                    dve.wait_ge(lexp_rdy, r.at(1, 1))
                    tt(gm[:, :, :], lexp[:, :, :], mask[:, :, :], ALU.mult).then_inc(route0, 1)
                if a:
                    dve.wait_ge(rz_rdy, a.at(1, 1))
                    dve.wait_ge(ldx[a.par], a.half(32, 32))
                    for k in range(TT):
                        stt(pre[:, k, :], o_ps[:, k, 0:D], rz[:, k:k + 1], xt[a.par][:, k, :], ALU.mult, ALU.add
                            ).then_inc(pre_rdy, 1)
                    dve.wait_ge(pre_rdy, a.at(TT, TT))
                    stats_of(pre, stats, mv, ve, a, ve_rdy)
                if r:
                    dve.wait_ge(route0, r.at(15, 12))
                    dve.tensor_reduce(gs[:, :], gm[:, :, :], AX.X, ALU.add).then_inc(route0, 1)
                    dve.wait_ge(route0, r.at(15, 13))
                    dve.reciprocal(gr[:, :], gs[:, :]).then_inc(route0, 1)
                    dve.wait_ge(route0, r.at(15, 14))
                    tt(xg[r.par][:, :, D:XGW], gm[:, :, :], col(gr, E0), ALU.mult).then_inc(route0, 1)
                    dve.wait_ge(d_mm, r.at(1, 1))
                    need(dve, st_r, r.at(16))
                    tt(resid[:, :, :], blk4(d_ps), xg[r.par][:, :, 0:D], ALU.add).then_inc(resid_rdy, 1)
                if a:
                    need(dve, st_xg[a.par], a.half(16))
                    need(dve, t_mm, a.at(1, -1))
                    normalise(xg[a.par], pre, mv, rstd, a, rstd_rdy, x1_rdy)

            stage1(Seq(0, 0), None)
            with dve.Fori(0, NB // 2 - 1) as j:
                for i in (1, 2):
                    stage1(Seq(j, i), Seq(j, i - 1))
            stage1(Seq(0, NB - 1), Seq(0, NB - 2))
            stage1(None, Seq(0, NB - 1))

            def take(src, dst, got):
                for c in range(CAP // 8):
                    got_c = dst[:, c * 8:(c + 1) * 8]
                    if c:
                        dve.wait_ge(taken, take_n[0])
                    dve.max(got_c, src).then_inc(got, 1)
                    dve.wait_ge(got, c + 1)
                    if c < CAP // 8 - 1:
                        dve.match_replace(src, got_c, src, 0.0).then_inc(taken, 1)
                        take_n[0] += 1

            take_n = [0]
            dve.wait_ge(seg_loaded, 16 * NSEG)
            tt(val[:, :], val[:, :], rev[:, :], ALU.mult).then_inc(val_rdy, 1)
            dve.wait_ge(val_rdy, 1)
            take(val[:, :], cand, cand_rdy)
            dve.wait_ge(cand_loaded, 16)
            take(cval[:, :], first, first_rdy)
            stt(empty[:, :], first[:, :], 0.0, slot_no[:, :], ALU.is_equal, ALU.mult).then_inc(empty_rdy, 1)
            dve.wait_ge(empty_rdy, 1)
            tt(idxf[:, :], empty[:, :], first[:, :], ALU.subtract).then_inc(idxd_rdy, 1)
            dve.wait_ge(idxd_rdy, 1)
            ts(idxf[:, :], idxf[:, :], float(TOK), None, ALU.add).then_inc(idxf_rdy, 1)
            dve.wait_ge(idx_mm, 1)
            dve.tensor_copy(idx[:, :], bank[6][:, 0:E0]).then_inc(idx_rdy, 1)

            def group(s):
                dve.wait_ge(te_rdy, s.at(1, 1))
                stt(se[:, :, :], te[:, :, :], 1.0, blk4(bank[3])[:, :, 0:I0], ALU.add, ALU.mult).then_inc(se_rdy, 1)
                dve.wait_ge(xe_got[s.par], s.half(16 * EG, 16 * EG))
                need(dve, ye_rdy, s.at(1))
                for k in range(EG):
                    dve.tensor_copy(ge[:, k:k + 1], xe[s.par][:, k, bass.ds(s.at(EG, D + k), 1)]).then_inc(ge_rdy, 1)
                dve.wait_ge(se_rdy, s.at(1, 1))
                need(dve, aeT_mm, s.at(1))
                stt(ae[:, :, :], se[:, :, :], 0.5, blk4(bank[3])[:, :, I0:2 * I0], ALU.mult, ALU.mult).then_inc(ae_rdy, 1)
                dve.wait_ge(dn_mm, s.at(1, 1))
                dve.wait_ge(ge_rdy, s.at(EG, EG))
                need(dve, added, s.at(16 * EG, -16 * EG))
                tt(ye[s.par][:, :, :], blk4(bank[5]), ge[:, :].rearrange("p (k e) -> p k e", e=1).to_broadcast([P, EG, D]),
                   ALU.mult).then_inc(ye_rdy, 1)

            group(Seq(0, 0))
            group(Seq(0, 1))
            with dve.Fori(1, E0 // EG // 2) as j:
                for i in (0, 1):
                    group(Seq(j, i))

            def conv(s, h):
                w, b = wt["convw"], wt["convb"]
                dve.wait_ge(xib_rdy, s.at(NH, h + 1))
                need(dve, xc_rdy, s.at(1))
                ts(cv[:, h, :], xib[:, h, 3:SEQ + 3], w[:, h, 3:4], b[:, h:h + 1], ALU.mult, ALU.add).then_inc(cv_rdy, 1)
                for k in range(3):
                    dve.wait_ge(cv_rdy, s.at(8, 4 * h + k + 1))
                    stt(cv[:, h, :], xib[:, h, k:k + SEQ], w[:, h, k:k + 1], cv[:, h, :], ALU.mult, ALU.add
                        ).then_inc(cv_rdy, 1)

            def front(s, n):
                if n == 2:
                    dve.wait_ge(ld_r, s.at(16, 16))
                    stats_of(rin, st1, mv1, ve1, s, f_ve)
                if n == 3:
                    need(dve, x3p_rdy, s.at(1, -1))
                    normalise(x2[s.par], rin, mv1, rs1, s, f_rs, x2_rdy)
                if n in (6, 7):
                    conv(s, n - 6)
                if n in (8, 9):
                    h = n - 8
                    dve.wait_ge(zc_rdy, s.at(NH, h + 1))
                    need(dve, y2_rdy, s.at(1, -1))
                    stt(zs[s.par][:, h, :], tz[:, h, :], 1.0, zc[:, h, :], ALU.add, ALU.mult).then_inc(zs_rdy, 1)
                if n == 10:
                    dve.wait_ge(tc_rdy, s.at(NH, NH))
                    need(dve, yd_rdy, s.at(NH, -NH))
                    stt(xc[s.par][:, :, :], tc[:, :, :], 1.0, cv[:, :, :], ALU.add, ALU.mult).then_inc(xc_rdy, 1)
                if n == 12:
                    dve.wait_ge(xpf_rdy, s.at(1, 1))
                    tt(rest1[:, :], xpf[:, :], parts[s.par][:, :], ALU.subtract).then_inc(rest_rdy, 1)
                    dve.wait_ge(rest_rdy, s.at(1, 1))
                    dve.tensor_copy(parts[s.par][32:64, :], rest1[32:64, :]).then_inc(parts2, 1)
                    dve.tensor_copy(mid[64:96, :], rest1[64:96, :]).then_inc(mid_rdy, 1)
                if n == 13:
                    dve.wait_ge(mid_rdy, s.at(1, 1))
                    dve.wait_ge(parts2, s.at(1, 1))
                    tt(parts[s.par][64:96, :], rest1[64:96, :], mid[64:96, :], ALU.subtract).then_inc(parts_rdy, 1)
                if n == 14:
                    dve.wait_ge(dtl_rdy, s.at(1, 1))
                    need(dve, da_rdy, s.at(NS * NH, -NS * NH))
                    need(dve, u_rdy, s.at(1, -1))
                    stt(dt_[s.par][:, :, :], dtp[:, :, :], 0.0, dta[:, :, :], ALU.max, ALU.add).then_inc(dt_rdy, 1)

            over_h = lambda b: b[:, :].rearrange("p (h t) -> p h t", h=1).to_broadcast([P, NH, SEQ])
            flat = lambda a: a[:, :, :].rearrange("p h t -> p (h t)")

            def gate(s, c):
                k = rows_of(c)
                dve.wait_ge(ha_rdy, s.at(NCH, c + 1))
                dve.wait_ge(h3_mm, s.at(NCH, c + 1))
                stt(hg[c % 2][0:k, :], h3_ps[0:k, :], wt["b3"][0:k, c:c + 1], ha[0:k, :], ALU.add, ALU.mult).then_inc(hg_rdy, 1)

            def silu(s, c):
                k = rows_of(c)
                dve.wait_ge(ht_rdy, s.at(NCH, c + 1))
                if c in (2, 3):
                    dve.wait_ge(dn_done, s.at(NCH, c - 1))
                stt(hs[c % 2][0:k, :], ht[c % 2][0:k, :], 1.0, hg[c % 2][0:k, :], ALU.add, ALU.mult).then_inc(hs_rdy, 1)

            def weigh(s, c):
                dve.wait_ge(hs_rdy, s.at(NCH, c + 1))
                dve.wait_ge(rwb_mm, s.at(RT_CH, c - SH_CH + 1))
                dve.wait_ge(dn_done, s.at(NCH, c - 1))
                tt(hh[c % 2][:, :], hs[c % 2][:, :], px_ps[:, :], ALU.mult).then_inc(hh_rdy, 1)

            def experts(s, n):
                if n == 0:
                    dve.wait_ge(y_mm, s.at(NS, NS))
                    need(dve, y2_rdy, s.at(1))
                    for h in range(NH):
                        stt(yd[:, h, :], xc[s.par][:, h, :], wt["dskip"][:, h:h + 1], y_ps[:, h, :], ALU.mult, ALU.add
                            ).then_inc(yd_rdy, 1)
                if n == 2:
                    dve.wait_ge(op_mm, s.at(1, 1))
                    tt(x3p[:, :, :], blk4(h1_ps), x2[s.par][:, :, :], ALU.add).then_inc(x3p_rdy, 1)
                    dve.wait_ge(x3p_rdy, s.at(1, 1))
                    stats_of(x3p, st2, mv2, ve2, s, m_ve)
                if n == 3:
                    normalise(x3[s.par], x3p, mv2, rs2, s, m_rs, x3_rdy)
                if n == 4:
                    dve.wait_ge(l1_rdy, s.at(1, 1))
                    dve.tensor_reduce(l1m[:, :], l1[:, :, :], AX.X, ALU.max).then_inc(route1, 1)
                    dve.wait_ge(route1, s.at(16, 1))
                    tt(l1s[:, :, :], l1[:, :, :], col(l1m, E1), ALU.subtract).then_inc(route1, 1)
                if n == 5:
                    dve.wait_ge(l1e_rdy, s.at(1, 1))
                    dve.tensor_reduce(l1z[:, :], l1e[:, :, :], AX.X, ALU.add).then_inc(route1, 1)
                    dve.wait_ge(route1, s.at(16, 3))
                    dve.reciprocal(l1r[:, :], l1z[:, :]).then_inc(route1, 1)
                    dve.wait_ge(route1, s.at(16, 4))
                    tt(sc1[:, :, :], l1e[:, :, :], col(l1r, E1), ALU.mult).then_inc(route1, 1)
                    dve.wait_ge(route1, s.at(16, 5))
                    tt(bi1[:, :, :], sc1[:, :, :], wt["gb1"][:, :].rearrange("p (t e) -> p t e", t=1).to_broadcast([P, TT, E1]),
                       ALU.add).then_inc(route1, 1)
                    dve.wait_ge(route1, s.at(16, 6))
                    settle(dve)
                    for k in range(TT):
                        dve.max(tp1[:, k, :], bi1[:, k, :]).then_inc(route1, 1)
                    dve.wait_ge(route1, s.at(16, 10))
                    settle(dve)
                    for k in range(TT):
                        dve.max_index(ti1[:, k, :], tp1[:, k, :], bi1[:, k, :]).then_inc(route1, 1)
                    dve.wait_ge(route1, s.at(16, 14))
                    one_hot(ho1, ti1, 2, E1).then_inc(route1, 1)
                    dve.wait_ge(route1, s.at(16, 15))
                    tt(hm1[:, :, :], ho1[:, :, 0, :], ho1[:, :, 1, :], ALU.add).then_inc(route1, 1)
                    dve.wait_ge(route1, s.at(16, 16))
                    need(dve, rwT_mm, s.at(1))
                    tt(rw[:, :, 0:E1], sc1[:, :, :], hm1[:, :, :], ALU.mult).then_inc(rw_rdy, 1)

            def tail(s, n):
                if n == 2:
                    dve.wait_ge(b2_mm, s.at(1, 1))
                    tt(of[:, :, :], blk4(fo_ps), x3[s.par][:, :, :], ALU.add).then_inc(of_rdy, 1)
                    dve.wait_ge(of_rdy, s.at(1, 1))
                    stats_of(of, st3, mv3, ve3, s, o_ve)
                if n == 4:
                    need(dve, st_o, s.at(16))
                    normalise(ofin, of, mv3, rs3, s, o_rs, ofin_rdy)

            def iteration(f, s, m, o):
                for n in range(NS):
                    c = n - 4
                    if s:
                        if n == 0:
                            dve.wait_ge(u_rdy, s.at(1, 1))
                        dve.wait_ge(bb_rdy, s.at(NS, n + 1))
                        tt(dbx[:, :, :], u[s.par][:, :, :], over_h(bb_ps), ALU.mult).then_inc(dbx_rdy, 1)
                    if m and c >= 1:
                        silu(m, c - 1)
                    if o and n < 2:
                        silu(o, NCH - 2 + n)
                    if s:
                        dve.wait_ge(dbx_rdy, s.at(NS, n + 1))
                        dve.wait_ge(da_rdy, s.at(NS * NH, NH * (n + 1)))
                        dve.tensor_tensor_scan(flat(hst), flat(dA[n % 2]), flat(dbx), 0.0, ALU.mult, ALU.add).then_inc(scan_rdy, 1)
                    if o and n == 0:
                        gate(o, NCH - 1)
                    if m and c >= 0:
                        gate(m, c)
                    if s:
                        dve.wait_ge(scan_rdy, s.at(NS, n + 1))
                        dve.wait_ge(cb_rdy, s.at(NS, n + 1))
                        need(dve, y_mm, s.at(NS, n - 1))
                        tt(prod[n % 2][:, :, :], hst[:, :, :], over_h(cb_ps), ALU.mult).then_inc(prod_rdy, 1)
                    if m:
                        experts(m, n)
                    if o:
                        tail(o, n)
                    if f:
                        front(f, n)
                    if m and c - 1 >= SH_CH:
                        weigh(m, c - 1)
                    if o and n < 2:
                        weigh(o, NCH - 2 + n)

            dve.wait_ge(added, E0 * 16)
            dve.memset(rw[:, :, E1:E1 + 1], 1.0)
            dve.memset(xib[:, :, 0:3], 0.0)
            for k in range(2):
                dve.memset(dA[k][:, :, 0:1], 0.0).then_inc(dve_init, 1)
            dve.wait_ge(dve_init, 4)
            schedule(dve, iteration)


def kernel(**inputs):
    import numpy as np
    import concourse.bacc as bacc
    from concourse.bass_utils import run_bass_kernel_spmd

    g = {k: np.asarray(v) for k, v in inputs.items()}
    c = np.ascontiguousarray

    def halves(a):
        return c(np.moveaxis(a.reshape(NH, P, *a.shape[1:]), 0, 1))

    def chunks(shared, routed):
        pad = np.zeros((D, SH_CH * P - H1), np.float32)
        return c(np.concatenate([shared, pad, np.moveaxis(routed, 0, 1).reshape(D, -1)], 1).reshape(D, NCH, P))

    def bias_chunks(shared, routed):
        pad = np.zeros(SH_CH * P - H1, np.float32)
        return c(np.concatenate([shared, pad, routed.reshape(-1)]).reshape(NCH, P).T)

    x = g["L0_attn_x"].reshape(TOK, D)
    W = g["L0_attn_W"]
    xp = g["L1_attn_x_proj_w"]
    bc = halves(xp[1:].T)
    w2 = np.concatenate([g["L1_ffn_sw2"], np.zeros((SH_CH * P - H1, D), np.float32), g["L1_ffn_w2"].reshape(-1, D)], 0)
    t = {
        "x": x, "xT": c(x.T), "Wq": c(W[:, :D]), "Wkv": c(W[:, D:]), "gw0": c(g["L0_ffn_gate_w"].T),
        "wgu": c(np.moveaxis(g["L0_ffn_w_gate_up"], 0, 1)), "wd": c(np.moveaxis(g["L0_ffn_w_down"], 0, 1)),
        "sgu": g["L0_ffn_shared_w_gate_up"], "sd": g["L0_ffn_shared_w_down"],
        "inp": c(g["L1_attn_in_proj_w"].T), "convw": halves(g["L1_attn_conv_w"][:, 0]), "convb": halves(g["L1_attn_conv_b"]),
        "xpw": c(np.concatenate([bc, bc, bc, np.zeros((P, NH, 32), np.float32)], 2)),
        "dtrow": c(np.broadcast_to(halves(xp[0])[:, :, None], (P, NH, P))),
        "dtw": halves(g["L1_attn_dt_proj_w"][:, 0]), "dtb": halves(g["L1_attn_dt_proj_b"]),
        "alog": halves(g["L1_attn_A_log"]), "dskip": halves(g["L1_attn_D"]), "outp": halves(g["L1_attn_out_proj_w"].T),
        "gw1": c(g["L1_ffn_gate_w"].T), "gb1": c(np.broadcast_to(g["L1_ffn_gate_b"], (P, E1))),
        "w1": chunks(g["L1_ffn_sw1"], g["L1_ffn_w1"]), "w3": chunks(g["L1_ffn_sw3"], g["L1_ffn_w3"]),
        "b1": bias_chunks(g["L1_ffn_sb1"], g["L1_ffn_b1"]), "b3": bias_chunks(g["L1_ffn_sb3"], g["L1_ffn_b3"]),
        "w2": c(np.moveaxis(w2.reshape(NCH, P, D), 0, 1)),
        "b2x": c(np.concatenate([g["L1_ffn_b2"], g["L1_ffn_sb2"][None]], 0)),
    }
    nc = bacc.Bacc("TRN2", target_bir_lowering=False, num_devices=1)
    arrays = {f"in_{n}": c(a) for n, a in t.items()}
    ins = {n: nc.dram_tensor(f"in_{n}", a.shape, F32, kind="ExternalInput").ap() for n, a in t.items()}
    out = nc.dram_tensor("out_dram", (TOK, D), F32, kind="ExternalOutput").ap()
    build(nc, ins, out)
    r = run_bass_kernel_spmd(nc, [arrays], core_ids=[0])
    return r.results[0]["out_dram"].reshape(NB, SEQ, D)
```

```python
from contextlib import ExitStack

import concourse.bass as bass
from concourse import mybir

F32 = mybir.dt.float32
BF16 = mybir.dt.bfloat16
U32 = mybir.dt.uint32
ALU = mybir.AluOpType
ACT = mybir.ActivationFunctionType
AX = mybir.AxisListType

P = 128
NB, SEQ, D = 16, 512, 128
DCONV = 4
TOK = NB * SEQ
TT = SEQ // P
E0, TOPK, CAP, I0 = 32, 4, 128, 64
XGW = D + E0
NSEG = 4
N_EARLY = 5 + NSEG
N_CONST = N_EARLY + 13
SEG = TOK // NSEG
DI, NH, NS = 256, 2, 16
NXP = 1 + 2 * NS
E1, H1 = 8, 176
SH_CH = 2
RT_CH = E1 * H1 // P
NCH = SH_CH + RT_CH
LN_EPS = 1e-5
Z_EPS = 1e-6
EG = 4
PAIRS = (3, 10, 12)
NADD = NS - len(PAIRS)
LATE = (7, 8, 9)
EARLY = ("Wkv", "Wq", "sgu", "gw0", "sd")
M0 = 5
TAIL = NCH - (NS - M0)


class Seq:

    def __init__(self, j, off):
        self.j, self.off, self.par = j, off, off % 2

    def at(self, per, k=0):
        return self.j * (2 * per) + (self.off * per + k)

    def half(self, per, k=0):
        return self.j * per + (self.off // 2 * per + k)


def need(eng, sem, value):
    if isinstance(value, int) and value <= 0:
        return
    eng.wait_ge(sem, value)


def sums_to(n):
    return n + 1 - sum(a < n for a in PAIRS)


def schedule(eng, iteration):
    q = lambda b: Seq(0, b) if 0 <= b < NB else None
    for i in range(-1, 2):
        iteration(q(i + 1), q(i), q(i - 1), None, q(i + 2))
    with eng.Fori(0, NB // 2 - 2) as j:
        for i in (2, 3):
            iteration(Seq(j, i + 1), Seq(j, i), Seq(j, i - 1), Seq(j, i - 2), Seq(j, i + 2))
    for i in range(NB - 2, NB + 2):
        iteration(q(i + 1), q(i), q(i - 1), q(i - 2), q(i + 2))


def build(nc, t, out):
    ctx = ExitStack()
    with ctx:
        def sb(name, shape, dt=F32):
            return ctx.enter_context(nc.sbuf_tensor(name, shape, dt))

        def sem(name):
            return ctx.enter_context(nc.semaphore(name))

        xg_d = nc.dram_tensor("xg_rows", (TOK + P, XGW), F32).ap()
        r_d = nc.dram_tensor("resid_rows", (TOK + P, D), F32).ap()
        mask_d = nc.dram_tensor("mask_by_expert", (E0, TOK), F32).ap()
        r2_d = nc.dram_tensor("resid_rows_2", (TOK + P, D), F32).ap()

        bank01 = ctx.enter_context(nc.psum_tensor("bank01", [P, 2, 512], F32))
        bank = {n: ctx.enter_context(nc.psum_tensor(f"bank{n}", [P, 512], F32)) for n in range(2, 8)}

        ident = sb("ident", [P, P])
        sel_bc = sb("sel_bc", [3 * NXP, NXP, P], BF16)
        sel_rw = sb("sel_rw", [96, RT_CH, P], BF16)
        identb = sb("identb", [P, P], BF16)
        iota_e = sb("iota_e", [P, E0])
        neghalf = sb("neghalf", [P, TT])
        slot_no = sb("slot_no", [E0, P])

        inc = sb("inc", [P, DCONV, DI])
        wt = {n: sb("w_" + n, list(t[n].shape)) for n in (
            "Wq", "Wkv", "gw0", "sgu", "sd", "inp", "convb", "xpw", "dtw", "dtb",
            "alog", "dskip", "outp", "gw1", "gb1", "w1", "w3", "b1", "b3", "w2", "b2x")}

        aneg = sb("aneg", [P, NH, NS])

        W_ALL = 16 * (len(wt) - len(EARLY) + 3)

        with ExitStack() as early:
            def eb(name, shape, dt=F32):
                return early.enter_context(nc.sbuf_tensor(name, shape, dt))

            convw = eb("w_convw", list(t["convw"].shape))
            wgu, wd = eb("w_wgu", list(t["wgu"].shape)), eb("w_wd", list(t["wd"].shape))
            xt = [eb(f"xt{p}", [P, TT, D]) for p in range(2)]
            xT = [eb(f"xT{p}", [P, SEQ]) for p in range(2)]
            ek = eb("ek", [P, TT, D])
            rk = eb("rk", [P, TT, D])
            kf = eb("kf", [P, TT, D])
            eq = eb("eq", [P, SEQ])
            rq = eb("rq", [P, SEQ])
            qf = eb("qf", [P, SEQ])
            vext = eb("vext", [P, TT, D + 1])
            kvx = eb("kvx", [P, D + 1])
            den = eb("den", [P, TT])
            rz = eb("rz", [P, TT])
            pre = eb("pre", [P, TT, D])
            xg = [eb(f"xg{p}", [P, TT, XGW]) for p in range(2)]
            x1T = eb("x1T", [P, SEQ])
            tg = eb("tg", [I0, SEQ])
            sg = eb("sg", [I0, SEQ])
            hsh = eb("hsh", [I0, SEQ])
            lg = eb("lg", [P, TT, E0])
            top = eb("top", [P, TT, 8])
            topi = eb("topi", [P, TT, 8], U32)
            lsub = eb("lsub", [P, TT, E0])
            lexp = eb("lexp", [P, TT, E0])
            hot = eb("hot", [P, TT, TOPK, E0])
            mask = eb("mask", [P, TT, E0])
            gm = eb("gm", [P, TT, E0])
            gs = eb("gs", [P, TT])
            gr = eb("gr", [P, TT])
            resid = eb("resid", [P, TT, D])
            maskT = eb("maskT", [E0, SEQ])
            zero = eb("zero", [P, XGW])
            stats = eb("stats", [P, TT, 6])
            mv = eb("mv", [P, TT, 2])
            rstd = eb("rstd", [P, TT])

            rev = eb("rev", [P, SEG])
            val = eb("val", [P, SEG])
            cand = eb("cand", [P, P])
            cval = eb("cval", [E0, NSEG * P])
            first = eb("first", [E0, P])
            empty = eb("empty", [E0, P])
            idxf = eb("idxf", [E0, P])
            idx = eb("idx", [P, E0], U32)

            xe = [eb(f"xe{p}", [P, EG, XGW]) for p in range(2)]
            ixg = [eb(f"ixg{p}", [P, EG], U32) for p in range(2)]
            ixs = [eb(f"ixs{p}", [P, EG], U32) for p in range(2)]
            xeT = eb("xeT", [P, EG, P])
            te = eb("te", [P, EG, I0])
            se = eb("se", [P, EG, I0])
            ae = eb("ae", [P, EG, I0])
            aeT = eb("aeT", [I0, EG, P])
            ge = eb("ge", [P, EG])
            ye = [eb(f"ye{p}", [P, EG, D]) for p in range(2)]


        rin = sb("rin", [P, TT, D])
        x2 = [sb(f"x2_{p}", [P, TT, D]) for p in range(2)]
        x2T = sb("x2T", [P, DCONV - 1 + SEQ])
        cv = sb("cv", [P, NH, SEQ])
        tc = sb("tc", [P, NH, SEQ])
        xc = [sb(f"xc{p}", [P, NH, SEQ]) for p in range(2)]
        tz = sb("tz", [P, NH, SEQ])
        zc = sb("zc", [P, NH, SEQ])
        zs = [sb(f"zs{p}", [P, NH, SEQ]) for p in range(2)]
        parts = [sb(f"parts{p}", [3 * NXP, SEQ], BF16) for p in range(2)]
        xpf = sb("xpf", [P, TT, NXP])
        xpr = sb("xpr", [P, TT, NXP])
        xpp = sb("xpp", [P, TT, 3 * NXP], BF16)
        dtp = sb("dtp", [P, NH, SEQ])
        dta = sb("dta", [P, NH, SEQ])
        dt_ = [sb(f"dt{p}", [P, NH, SEQ]) for p in range(2)]
        bs = [sb(f"bs{p}", [P, SEQ]) for p in range(2)]
        u = [sb(f"u{p}", [P, NH, SEQ]) for p in range(2)]
        dA = [sb(f"dA{k}", [P, NH, SEQ]) for k in range(2)]
        dbx = [sb(f"dbx{k}", [P, NH, SEQ]) for k in range(2)]
        hst = [sb(f"hst{k}", [P, NH, SEQ]) for k in range(2)]
        prod = [sb(f"prod{k}", [P, NH, SEQ]) for k in range(2)]
        yd = sb("yd", [P, NH, SEQ])
        y2 = sb("y2", [P, NH, SEQ])
        x3p = sb("x3p", [P, TT, D])
        x3 = [sb(f"x3_{p}", [P, TT, D]) for p in range(2)]
        x3T = sb("x3T", [P, SEQ])
        l1 = sb("l1", [P, TT, E1])
        l1m = sb("l1m", [P, TT])
        l1s = sb("l1s", [P, TT, E1])
        l1e = sb("l1e", [P, TT, E1])
        l1z = sb("l1z", [P, TT])
        l1r = sb("l1r", [P, TT])
        sc1 = sb("sc1", [P, TT, E1])
        bi1 = sb("bi1", [P, TT, E1])
        tp1 = sb("tp1", [P, TT, 8])
        ti1 = sb("ti1", [P, TT, 8], U32)
        ho1 = sb("ho1", [P, TT, 2, E1])
        hm1 = sb("hm1", [P, TT, E1])
        rw = sb("rw", [P, TT, E1 + 1])
        rwr = sb("rwr", [P, TT, E1 + 1])
        rwp = sb("rwp", [P, TT, 96], BF16)
        rwT = [sb(f"rwT{p}", [96, SEQ]) for p in range(2)]
        rwTb = [sb(f"rwTb{p}", [96, SEQ], BF16) for p in range(2)]
        ha = sb("ha", [P, SEQ])
        hg = [sb(f"hg{k}", [P, SEQ]) for k in range(2)]
        ht = [sb(f"ht{k}", [P, SEQ]) for k in range(2)]
        hs = [sb(f"hs{k}", [P, SEQ]) for k in range(2)]
        hh = [sb(f"hh{k}", [P, SEQ]) for k in range(2)]
        of = sb("of", [P, TT, D])
        ofin = sb("ofin", [P, TT, D])
        st1 = sb("st1", [P, TT, 6])
        mv1 = sb("mv1", [P, TT, 2])
        rs1 = sb("rs1", [P, TT])
        st2 = sb("st2", [P, TT, 6])
        mv2 = sb("mv2", [P, TT, 2])
        rs2 = sb("rs2", [P, TT])
        st3 = sb("st3", [P, TT, 6])
        mv3 = sb("mv3", [P, TT, 2])
        rs3 = sb("rs3", [P, TT])

        w_loaded, const_rdy, half_rdy, a_exp, zeros_stored = sem("w_loaded"), sem("const_rdy"), sem("half_rdy"), sem("a_exp"), sem("zeros_stored")
        dve_init = sem("dve_init")
        ldx0, ldx1, kv_mm, q_mm, ek_rdy = sem("ldx0"), sem("ldx1"), sem("kv_mm"), sem("q_mm"), sem("ek_rdy")
        v_rdy, rk_rdy, kf_rdy, eq_rdy, rq_rdy = sem("v_rdy"), sem("rk_rdy"), sem("kf_rdy"), sem("eq_rdy"), sem("rq_rdy")
        qf_rdy = sem("qf_rdy")
        kva_mm, kvx_rdy, o_mm, den_rdy, rz_rdy = sem("kva_mm"), sem("kvx_rdy"), sem("o_mm"), sem("den_rdy"), sem("rz_rdy")
        pre_rdy, mv_rdy, rstd_rdy = sem("pre_rdy"), sem("mv_rdy"), sem("rstd_rdy")
        x1_rdy = sem("x1_rdy")
        t_mm, x1T_rdy, gu_mm, l_mm, lg_rdy = sem("t_mm"), sem("x1T_rdy"), sem("gu_mm"), sem("l_mm"), sem("lg_rdy")
        tg_rdy, sg_rdy, hsh_rdy = sem("tg_rdy"), sem("sg_rdy"), sem("hsh_rdy")
        lexp_rdy = sem("lexp_rdy")
        d_mm, mt_mm = sem("d_mm"), sem("mt_mm")
        maskT_rdy, resid_rdy, st_xg0, st_xg1, st_r = sem("maskT_rdy"), sem("resid_rdy"), sem("st_xg0"), sem("st_xg1"), sem("st_r")
        st_m = sem("st_m")
        seg_loaded, val_rdy, cand_rdy, ld_r2, cand_loaded = sem("seg_loaded"), sem("val_rdy"), sem("cand_rdy"), sem("ld_r2"), sem("cand_loaded")
        first_rdy, empty_rdy, idxf_rdy, idx_mm, idx_rdy = sem("first_rdy"), sem("empty_rdy"), sem("idxf_rdy"), sem("idx_mm"), sem("idx_rdy")
        xe_got0, xe_got1, xeT_mm, xeT_rdy, gu_e = sem("xe_got0"), sem("xe_got1"), sem("xeT_mm"), sem("xeT_rdy"), sem("gu_e")
        te_rdy, se_rdy, ae_rdy, aeT_mm, aeT_rdy = sem("te_rdy"), sem("se_rdy"), sem("ae_rdy"), sem("aeT_mm"), sem("aeT_rdy")
        dn_mm, ge_rdy, ye_rdy, added = sem("dn_mm"), sem("ge_rdy"), sem("ye_rdy"), sem("added")
        ld_r, f_mv, f_rs = sem("ld_r"), sem("f_mv"), sem("f_rs")
        x2_rdy, x2T_mm, x2T_rdy, cv_mm, bs_rdy = sem("x2_rdy"), sem("x2T_mm"), sem("x2T_rdy"), sem("cv_mm"), sem("bs_rdy")
        cv_rdy = sem("cv_rdy")
        tc_rdy, xc_rdy, z_mm, tz_rdy, zs_rdy = sem("tc_rdy"), sem("xc_rdy"), sem("z_mm"), sem("tz_rdy"), sem("zs_rdy")
        xp_mm, split_rdy, parts_mm, parts_rdy = sem("xp_mm"), sem("split_rdy"), sem("parts_mm"), sem("parts_rdy")
        dtr_mm, dtp_rdy, dta_rdy, dte_rdy, dtl_rdy = sem("dtr_mm"), sem("dtp_rdy"), sem("dta_rdy"), sem("dte_rdy"), sem("dtl_rdy")
        dt_rdy, u_rdy = sem("dt_rdy"), sem("u_rdy")
        bb_rdy, cb_rdy, da_rdy, dbx_rdy, scan_rdy = sem("bb_rdy"), sem("cb_rdy"), sem("da_rdy"), sem("dbx_rdy"), sem("scan_rdy")
        prod_rdy, y_mm = sem("prod_rdy"), sem("y_mm")
        yd_rdy, y2_rdy, op_mm, x3p_rdy = sem("yd_rdy"), sem("y2_rdy"), sem("op_mm"), sem("x3p_rdy")
        m_mv, m_rs, x3_rdy, x3T_mm = sem("m_mv"), sem("m_rs"), sem("x3_rdy"), sem("x3T_mm")
        x3T_rdy, l1_mm, l1_rdy = sem("x3T_rdy"), sem("l1_mm"), sem("l1_rdy")
        l1e_rdy = sem("l1e_rdy")
        rwT_mm, rwT_rdy, h1_mm, h3_mm, ha_rdy = sem("rwT_mm"), sem("rwT_rdy"), sem("h1_mm"), sem("h3_mm"), sem("ha_rdy")
        hg_rdy, ht_rdy, hs_rdy, rwb_mm, hh_rdy = sem("hg_rdy"), sem("ht_rdy"), sem("hs_rdy"), sem("rwb_mm"), sem("hh_rdy")
        dn_done = sem("dn_done")
        of_rdy, o_mv, o_rs = sem("of_rdy"), sem("o_mv"), sem("o_rs")
        ofin_rdy, st_o = sem("ofin_rdy"), sem("st_o")
        zc_rdy, xpf_rdy, ixg_rdy, ixs_rdy = sem("zc_rdy"), sem("xpf_rdy"), sem("ixg_rdy"), sem("ixs_rdy")

        added2, pair_rdy, w_early, rwf_rdy, settled, b2_mm, taken, idxd_rdy, a_neg = sem("added2"), sem("pair_rdy"), sem("w_early"), sem("rwf_rdy"), sem("settled"), sem("b2_mm"), sem("taken"), sem("idxd_rdy"), sem("a_neg")
        route0, route1 = sem("route0"), sem("route1")

        ldx, st_xg, xe_got = [ldx0, ldx1], [st_xg0, st_xg1], [xe_got0, xe_got1]

        def settle(eng):
            eng.sem_inc(settled, 1)

        block = ctx.enter_context(nc.Block())

        kv_ps = bank01[:, :, :].rearrange("p a (b c) -> p (a b) c", b=2)
        o_ps = kv_ps
        q_ps, kva_ps, t_ps = bank[2], bank[3], bank[4]
        g_ps, u_ps, d_ps = bank[5], bank[6], bank[7]
        y_ps = bank01
        pa_ps, cb_ps, h1_ps, h3_ps, fo_ps, pv_ps = bank[2], bank[3], bank[4], bank[5], bank[6], bank[7]
        blk4 = lambda a: a[:, :].rearrange("p (t c) -> p t c", t=TT)
        sel_e = lambda c: sel_rw[:, c - SH_CH, :]
        rows_of = lambda c: H1 - P if c == 1 else P
        N1 = NB * TT

        @block.sync
        def _(sp):
            for n in EARLY:
                sp.dma_start(wt[n][:], t[n]).then_inc(w_early, 16)

            def load_x(s):
                for read, count in ((pre_rdy, s.at(TT, -TT)), (q_mm, s.at(1, -1))):
                    need(sp, read, count)
                    settle(sp)
                sp.dma_start(xt[s.par][:, :, :], t["x"][bass.ds(s.at(SEQ), SEQ), :].rearrange("(t p) d -> p t d", p=P)
                             ).then_inc(ldx[s.par], 16)
                sp.dma_start(xT[s.par][:, :], t["xT"][:, bass.ds(s.at(SEQ), SEQ)]).then_inc(ldx[s.par], 16)

            def store_routed(s):
                sp.dma_start(r2_d[bass.ds(s.at(SEQ), SEQ), :].rearrange("(t p) d -> p t d", p=P),
                             zero[:, 0:D].rearrange("p (t d) -> p t d", t=1).to_broadcast([P, TT, D])).then_inc(zeros_stored, 16)
                sp.wait_ge(resid_rdy, s.at(1, 1))
                sp.dma_start(r_d[bass.ds(s.at(SEQ), SEQ), :].rearrange("(t p) d -> p t d", p=P), resid[:, :, :]
                             ).then_inc(st_r, 16)
                sp.wait_ge(maskT_rdy, s.at(1, 1))
                settle(sp)
                sp.dma_start(mask_d[:, bass.ds(s.at(SEQ), SEQ)], maskT[:, :]).then_inc(st_m, 16)
                sp.wait_ge(route0, s.at(15, 15))
                sp.dma_start(xg_d[bass.ds(s.at(SEQ), SEQ), :].rearrange("(t p) d -> p t d", p=P), xg[s.par][:, :, :]
                             ).then_inc(st_xg[s.par], 16)

            load_x(Seq(0, 0))
            sp.dma_start(wgu[:], t["wgu"]).then_inc(w_loaded, 16)
            sp.dma_start(wd[:], t["wd"]).then_inc(w_loaded, 16)
            sp.dma_start(convw[:], t["convw"]).then_inc(w_loaded, 16)
            for n, w in wt.items():
                if n not in EARLY:
                    sp.dma_start(w[:], t[n]).then_inc(w_loaded, 16)
            sp.wait_ge(dve_init, 1)
            sp.dma_start(xg_d[TOK:TOK + P, :], zero[:, :]).then_inc(zeros_stored, 16)
            sp.dma_start(r_d[TOK:TOK + P, :], zero[:, 0:D]).then_inc(zeros_stored, 16)
            sp.dma_start(r2_d[TOK:TOK + P, :], zero[:, 0:D]).then_inc(zeros_stored, 16)
            load_x(Seq(0, 1))
            with sp.Fori(0, NB // 2 - 1) as j:
                for i in (1, 2):
                    load_x(Seq(j, i + 1))
                    store_routed(Seq(j, i - 1))
            store_routed(Seq(0, NB - 2))
            store_routed(Seq(0, NB - 1))

            sp.wait_ge(st_m, NB * 16)
            for k in range(NSEG):
                sp.dma_start(val[k * E0:(k + 1) * E0, :], mask_d[:, k * SEG:(k + 1) * SEG]).then_inc(seg_loaded, 16)
            sp.wait_ge(cand_rdy, CAP // 8)
            for k in range(NSEG):
                sp.dma_start(cval[:, k * P:(k + 1) * P], cand[k * E0:(k + 1) * E0, :]).then_inc(cand_loaded, 16)

            def load_r(s):
                need(sp, x2_rdy, s.at(TT))
                sp.dma_start(rin[:, :, :], r_d[bass.ds(s.at(SEQ), SEQ), :].rearrange("(t p) d -> p t d", p=P)
                             ).then_inc(ld_r, 16)

            def store_out(s):
                sp.wait_ge(ofin_rdy, s.at(TT, TT))
                sp.dma_start(out[bass.ds(s.at(SEQ), SEQ), :].rearrange("(t p) d -> p t d", p=P), ofin[:, :, :]
                             ).then_inc(st_o, 16)

            sp.wait_ge(added, E0 // 2 * 16)
            sp.wait_ge(added2, E0 // 2 * 16)
            load_r(Seq(0, 0))
            load_r(Seq(0, 1))
            load_r(Seq(0, 2))
            with sp.Fori(0, NB // 2 - 2) as j:
                for i in (2, 3):
                    load_r(Seq(j, i + 1))
                    store_out(Seq(j, i - 2))
            load_r(Seq(0, NB - 1))
            for b in range(NB - 4, NB):
                store_out(Seq(0, b))
            sp.wait_ge(st_o, NB * 16)

        @block.gpsimd
        def _(gp):
            made = [0]

            def make(ins):
                made[0] += 1
                ins.then_inc(const_rdy, 1)
                gp.wait_ge(const_rdy, made[0])

            make(gp.memset(ident[:, :], 0.0))
            make(gp.affine_select(out=ident[:, :], in_=ident[:, :], compare_op=ALU.not_equal, fill=1.0, base=0,
                                  pattern=[[-1, P]], channel_multiplier=1))
            make(gp.memset(neghalf[:, :], -0.5))
            make(gp.iota(iota_e[:, :], [[1, E0]], base=0, channel_multiplier=0, allow_small_or_imprecise_dtypes=True))
            make(gp.iota(slot_no[:, :], [[1, P]], base=0, channel_multiplier=0, allow_small_or_imprecise_dtypes=True))
            for k in range(NSEG):
                make(gp.iota(rev[k * E0:(k + 1) * E0, :], [[-1, SEG]], base=TOK - k * SEG, channel_multiplier=0,
                             allow_small_or_imprecise_dtypes=True))
            def rsqrt(dst, src, s, ready, done):
                gp.wait_ge(ready, s.at(8, 8))
                settle(gp)
                gp.tensor_scalar(dst[:, :], src[:, :, 1], LN_EPS, None, ALU.add).then_inc(done, 1)
                gp.wait_ge(done, s.at(2, 1))
                gp.tensor_tensor(dst[:, :], dst[:, :], neghalf[:, :], ALU.pow).then_inc(done, 1)

            rsqrt(rstd, mv, Seq(0, 0), mv_rdy, rstd_rdy)
            with gp.Fori(0, NB // 2 - 1) as j:
                for i in (1, 2):
                    rsqrt(rstd, mv, Seq(j, i), mv_rdy, rstd_rdy)
            rsqrt(rstd, mv, Seq(0, NB - 1), mv_rdy, rstd_rdy)

            for part in range(3):
                rows = sel_rw[32 * part:32 * part + 32, :, :]
                make(gp.memset(rows, 1.0))
                make(gp.affine_select(out=rows, in_=rows, compare_op=ALU.is_ge, fill=0.0, base=0,
                                      pattern=[[P, RT_CH], [1, P]], channel_multiplier=-H1))
                make(gp.affine_select(out=rows, in_=rows, compare_op=ALU.is_ge, fill=0.0, base=H1 - 1,
                                      pattern=[[-P, RT_CH], [-1, P]], channel_multiplier=H1))
            make(gp.memset(sel_bc[:, :, :], 0.0))
            for part in range(3):
                make(gp.affine_select(out=sel_bc[:, :, :], in_=sel_bc[:, :, :], compare_op=ALU.not_equal, fill=1.0,
                                      base=-part * NXP, pattern=[[-1, NXP], [0, P]], channel_multiplier=1))

            gp.wait_ge(idx_rdy, 1)
            for q in (0, 1):
                gp.wait_ge(st_xg[q], NB // 2 * 16)
            gp.wait_ge(st_r, NB * 16)
            gp.wait_ge(zeros_stored, (3 + NB) * 16)

            def take_indices(dst, s, done):
                gp.tensor_copy(dst[s.par][:, :], idx[:, bass.ds(s.at(EG), EG)]).then_inc(done, 1)

            def gather(s, k):
                gp.indirect_dma_start(xe[s.par][:, k, :], None, xg_d[:, :], bass.IndirectOffsetOnAxis(ixg[s.par][:, k:k + 1], 0)
                                      ).then_inc(xe_got[s.par], 16)

            def scatter(s, k):
                to, done = ((r_d, added), (r2_d, added2))[k % 2]
                need(gp, done, s.at(EG // 2 * 16, k // 2 * 16))
                settle(gp)
                gp.indirect_dma_start(to[:, :], bass.IndirectOffsetOnAxis(ixs[s.par][:, k:k + 1], 0), ye[s.par][:, k, :], None,
                                      compute_op=ALU.add).then_inc(done, 16)

            def group(s, ahead):
                gp.wait_ge(ye_rdy, s.at(1, 1))
                settle(gp)
                take_indices(ixs, s, ixs_rdy)
                if ahead:
                    take_indices(ixg, ahead, ixg_rdy)
                    gp.wait_ge(ixg_rdy, ahead.at(1, 1))
                gp.wait_ge(ixs_rdy, s.at(1, 1))
                settle(gp)
                for k in range(EG):
                    scatter(s, k)
                    if ahead:
                        gather(ahead, k)

            for i in (0, 1):
                take_indices(ixg, Seq(0, i), ixg_rdy)
                gp.wait_ge(ixg_rdy, i + 1)
                for k in range(EG):
                    gather(Seq(0, i), k)
            with gp.Fori(0, E0 // EG // 2 - 1) as j:
                for i in (0, 1):
                    group(Seq(j, i), Seq(j, i + 2))
            group(Seq(0, E0 // EG - 2), None)
            group(Seq(0, E0 // EG - 1), None)

            def split_gates(s):
                part = [rwp[:, :, 32 * k:32 * k + E1 + 1] for k in range(3)]
                gp.wait_ge(rwf_rdy, s.at(5, 1))
                need(gp, rwT_mm, s.at(1))
                settle(gp)
                gp.tensor_copy(part[0], rw[:, :, :]).then_inc(rwf_rdy, 1)
                gp.wait_ge(rwf_rdy, s.at(5, 2))
                gp.tensor_tensor(rwr[:, :, :], rw[:, :, :], part[0], ALU.subtract).then_inc(rwf_rdy, 1)
                gp.wait_ge(rwf_rdy, s.at(5, 3))
                settle(gp)
                gp.tensor_copy(part[1], rwr[:, :, :]).then_inc(rwf_rdy, 1)
                gp.wait_ge(rwf_rdy, s.at(5, 4))
                gp.tensor_tensor(part[2], rwr[:, :, :], part[1], ALU.subtract).then_inc(rwf_rdy, 1)

            def load_second(s):
                gp.wait_ge(ld_r, s.at(16, 16))
                settle(gp)
                gp.dma_start(rin[:, :, :], r2_d[bass.ds(s.at(SEQ), SEQ), :].rearrange("(t p) d -> p t d", p=P),
                             accum_op=ALU.add).then_inc(ld_r2, 16)

            def spread_u(s, n):
                if n == 0:
                    gp.wait_ge(u_rdy, s.at(1, 1))
                gp.wait_ge(bs_rdy, s.at(NS, n + 1))
                need(gp, scan_rdy, s.at(NS, n - 1))
                gp.tensor_tensor(dbx[n % 2][:, :, :], u[s.par][:, :, :],
                                 bs[n % 2][:, :].rearrange("p (h t) -> p h t", h=1).to_broadcast([P, NH, SEQ]), ALU.mult
                                 ).then_inc(dbx_rdy, 1)

            def iteration(f, s, m, o, ahead):
                for n in range(NS):
                    if s and n < NS - 1:
                        spread_u(s, n + 1)
                    if f and n == NS - 1:
                        spread_u(f, 0)
                    if m and n == 0:
                        gp.wait_ge(yd_rdy, m.at(NH, NH))
                        need(gp, op_mm, m.at(1))
                        gp.tensor_tensor(y2[:, :, :], yd[:, :, :], zs[m.par][:, :, :], ALU.mult).then_inc(y2_rdy, 1)
                    if m and n == 2:
                        rsqrt(rs2, mv2, m, m_mv, m_rs)
                    if m and n == M0 + 1:
                        split_gates(m)
                    if o and n == TAIL + 2:
                        rsqrt(rs3, mv3, o, o_mv, o_rs)
                    if f and n == NS - 2:
                        gp.wait_ge(dt_rdy, f.at(1, 1))
                        need(gp, dbx_rdy, f.at(NS, -NS))
                        gp.tensor_tensor(u[f.par][:, :, :], dt_[f.par][:, :, :], xc[f.par][:, :, :], ALU.mult).then_inc(u_rdy, 1)
                    if ahead and n == NS - 5:
                        load_second(ahead)
                    if ahead and n == NS - 1:
                        rsqrt(rs1, mv1, ahead, f_mv, f_rs)

            gp.wait_ge(added, E0 // 2 * 16)
            gp.wait_ge(added2, E0 // 2 * 16)
            load_second(Seq(0, 0))
            rsqrt(rs1, mv1, Seq(0, 0), f_mv, f_rs)
            schedule(gp, iteration)

        @block.scalar
        def _(act):
            def stage1(a, r):
                if a:
                    act.wait_ge(kv_mm, a.at(1, 1))
                    need(act, kf_rdy, a.at(1))
                    act.activation(ek[:, :, :], kv_ps[:, :, 0:D], ACT.Exp).then_inc(ek_rdy, 1)
                    need(act, kva_mm, a.at(1))
                    act.activation(vext[:, :, 0:D], kv_ps[:, :, D:2 * D], ACT.Copy).then_inc(v_rdy, 1)
                    act.wait_ge(q_mm, a.at(1, 1))
                    need(act, qf_rdy, a.at(1))
                    act.activation(eq[:, :], q_ps[:, :], ACT.Exp).then_inc(eq_rdy, 1)
                if r:
                    act.wait_ge(t_mm, r.at(1, 1))
                    need(act, gu_mm, r.at(1))
                    act.activation(x1T[:, :], t_ps[:, :], ACT.Copy).then_inc(x1T_rdy, 1)
                if r:
                    act.wait_ge(l_mm, r.at(1, 1))
                    need(act, route0, r.at(15))
                    act.activation(lg[:, :, :], t_ps[:, 0:TT * E0].rearrange("p (t e) -> p t e", t=TT), ACT.Copy
                                   ).then_inc(lg_rdy, 1)
                    act.wait_ge(gu_mm, r.at(1, 1))
                    need(act, sg_rdy, r.at(1))
                    act.activation(tg[:, :], g_ps[0:I0, :], ACT.Tanh).then_inc(tg_rdy, 1)
                if a:
                    act.wait_ge(kva_mm, a.at(1, 1))
                    need(act, o_mm, a.at(1))
                    act.activation(kvx[:, :], kva_ps[:, 0:D + 1], ACT.Copy).then_inc(kvx_rdy, 1)
                if r:
                    act.wait_ge(route0, r.at(15, 5))
                    need(act, route0, r.at(15))
                    act.activation(lexp[:, :, :], lsub[:, :, :], ACT.Exp).then_inc(lexp_rdy, 1)
                    act.wait_ge(mt_mm, r.at(1, 1))
                    need(act, st_m, r.at(16))
                    act.activation(maskT[:, :], kva_ps[0:E0, :], ACT.Copy).then_inc(maskT_rdy, 1)

            stage1(Seq(0, 0), None)
            with act.Fori(0, NB // 2 - 1) as j:
                for i in (1, 2):
                    stage1(Seq(j, i), Seq(j, i - 1))
            stage1(Seq(0, NB - 1), Seq(0, NB - 2))
            stage1(None, Seq(0, NB - 1))

            act.wait_ge(w_loaded, W_ALL)
            act.activation(aneg[:, :, :], wt["alog"][:, :, :], ACT.Exp).then_inc(a_exp, 1)

            def group(s):
                act.wait_ge(xeT_mm, s.at(1, 1))
                need(act, gu_e, s.at(1))
                act.activation(xeT[:, :, :], blk4(bank[2]), ACT.Copy).then_inc(xeT_rdy, 1)
                act.wait_ge(gu_e, s.at(1, 1))
                need(act, se_rdy, s.at(1))
                act.activation(te[:, :, :], blk4(bank[3])[:, :, 0:I0], ACT.Tanh, scale=0.5).then_inc(te_rdy, 1)
                act.wait_ge(aeT_mm, s.at(1, 1))
                need(act, dn_mm, s.at(1))
                act.activation(aeT[:, :, :], blk4(bank[4])[0:I0], ACT.Copy).then_inc(aeT_rdy, 1)

            with act.Fori(0, E0 // EG // 2) as j:
                for i in (0, 1):
                    group(Seq(j, i))

            def front(s, n):
                if n == 3:
                    act.wait_ge(x2T_mm, s.at(1, 1))
                    act.activation(x2T[:, DCONV - 1:], pv_ps[:, :], ACT.Copy).then_inc(x2T_rdy, 1)
                if n in (4, 6):
                    h = n // 2 - 2
                    act.wait_ge(cv_mm, s.at(NH, h + 1))
                    need(act, xc_rdy, s.at(1))
                    b = wt["convb"][:, h:h + 1]
                    act.activation(tc[:, h, :], pv_ps[:, :], ACT.Tanh, bias=b).then_inc(tc_rdy, 1)
                    act.activation(cv[:, h, :], pv_ps[:, :], ACT.Identity, bias=b).then_inc(cv_rdy, 1)
                if n in (7, 9):
                    h = (n - 7) // 2
                    act.wait_ge(z_mm, s.at(NH, h + 1))
                    need(act, zs_rdy, s.at(NH, h + 1 - NH))
                    act.activation(tz[:, h, :], pa_ps[:, :], ACT.Tanh).then_inc(tz_rdy, 1)
                    act.activation(zc[:, h, :], pa_ps[:, :], ACT.Copy).then_inc(zc_rdy, 1)
                if n == 8:
                    act.wait_ge(xp_mm, s.at(1, 1))
                    need(act, split_rdy, s.at(4))
                    act.activation(xpf[:, :, :], pa_ps[:, 0:TT * NXP].rearrange("p (t c) -> p t c", t=TT), ACT.Copy
                                   ).then_inc(xpf_rdy, 1)
                if n == 10:
                    act.wait_ge(parts_mm, s.at(1, 1))
                    need(act, cb_rdy, s.at(NS, -NS))
                    act.activation(parts[s.par][:, :], pa_ps[0:3 * NXP, :], ACT.Copy).then_inc(parts_rdy, 1)
                if n == 11:
                    act.wait_ge(dtr_mm, s.at(1, 1))
                    need(act, dt_rdy, s.at(1))
                    for h in range(NH):
                        act.activation(dtp[:, h, :], pa_ps[:, :], ACT.Identity, bias=wt["dtb"][:, h:h + 1],
                                       scale=wt["dtw"][:, h:h + 1]).then_inc(dtp_rdy, 1)
                    act.wait_ge(dtp_rdy, s.at(NH, NH))
                    act.activation(dta[:, :, :], dtp[:, :, :], ACT.Abs).then_inc(dta_rdy, 1)
                if n == 12:
                    act.wait_ge(dta_rdy, s.at(1, 1))
                    act.activation(dta[:, :, :], dta[:, :, :], ACT.Exp, scale=-1.0).then_inc(dte_rdy, 1)
                if n == 13:
                    act.wait_ge(dte_rdy, s.at(1, 1))
                    act.activation(dta[:, :, :], dta[:, :, :], ACT.Ln, bias=1.0).then_inc(dtl_rdy, 1)

            def copy_b(s, n):
                act.wait_ge(bb_rdy, s.at(NS, n + 1))
                need(act, dbx_rdy, s.at(NS, n - 1))
                act.activation(bs[n % 2][:, :], pa_ps[:, :], ACT.Copy).then_inc(bs_rdy, 1)

            def scan_step(s, n):
                if n == 0:
                    act.wait_ge(dt_rdy, s.at(1, 1))
                need(act, scan_rdy, s.at(NS, n - 1))
                for h in range(NH):
                    act.activation(dA[n % 2][:, h, 1:SEQ], dt_[s.par][:, h, 1:SEQ], ACT.Exp, scale=aneg[:, h, n:n + 1]
                                   ).then_inc(da_rdy, 1)

            def chunk_a(s, c):
                act.wait_ge(h1_mm, s.at(NCH, c + 1))
                need(act, hg_rdy, s.at(NCH, c))
                k = rows_of(c)
                act.activation(ha[0:k, :], h1_ps[0:k, :], ACT.Identity, bias=wt["b1"][0:k, c:c + 1]).then_inc(ha_rdy, 1)

            def chunk_t(s, c):
                act.wait_ge(hg_rdy, s.at(NCH, c + 1))
                need(act, hs_rdy, s.at(NCH, c - 1))
                k = rows_of(c)
                act.activation(ht[c % 2][0:k, :], hg[c % 2][0:k, :], ACT.Tanh).then_inc(ht_rdy, 1)

            def experts_a(s, n):
                if n == M0 - 1:
                    act.wait_ge(x3T_mm, s.at(1, 1))
                    act.activation(x3T[:, :], h3_ps[:, :], ACT.Copy).then_inc(x3T_rdy, 1)
                if n == M0:
                    act.wait_ge(l1_mm, s.at(1, 1))
                    act.activation(l1[:, :, :], pa_ps[:, 0:TT * E1].rearrange("p (t e) -> p t e", t=TT), ACT.Copy
                                   ).then_inc(l1_rdy, 1)
                if n == M0 + 1:
                    act.wait_ge(route1, s.at(16, 2))
                    act.activation(l1e[:, :, :], l1s[:, :, :], ACT.Exp).then_inc(l1e_rdy, 1)
                if n == M0 + 2:
                    act.wait_ge(rwT_mm, s.at(1, 1))
                    act.activation(rwT[s.par][:, :], pa_ps[0:96, :], ACT.Copy)
                    act.activation(rwTb[s.par][:, :], pa_ps[0:96, :], ACT.Copy).then_inc(rwT_rdy, 1)

            def iteration(f, s, m, o, ahead):
                for n in range(NS):
                    c = n - M0
                    if m and c >= 1:
                        chunk_t(m, c - 1)
                    if o and n <= TAIL:
                        chunk_t(o, NS - 1 - M0 + n)
                    if s and n < NS - 1:
                        scan_step(s, n + 1)
                    if f and n == NS - 1:
                        scan_step(f, 0)
                    if s and n < NS - 2:
                        copy_b(s, n + 2)
                    if f and n >= NS - 2:
                        copy_b(f, n + 2 - NS)
                    if o and n < TAIL:
                        chunk_a(o, NS - M0 + n)
                    if m and c >= 0:
                        chunk_a(m, c)
                    if m:
                        experts_a(m, n)
                    if f:
                        front(f, n)

            act.wait_ge(added, E0 // 2 * 16)
            act.wait_ge(added2, E0 // 2 * 16)
            act.wait_ge(half_rdy, 6 + DCONV)
            act.wait_ge(a_neg, 1)
            schedule(act, iteration)

        @block.tensor
        def _(pe):
            mm = pe.matmul
            tile = lambda k: slice(k * P, (k + 1) * P)
            pe.wait_ge(w_early, 16 * len(EARLY))
            pe.wait_ge(const_rdy, 2)
            pe.wait_ge(half_rdy, 1)
            pe.wait_ge(dve_init, 2)

            def stage1(a, r):
                if a:
                    pe.wait_ge(ldx[a.par], a.half(32, 32))
                    need(pe, pre_rdy, a.at(TT))
                    for k in range(TT):
                        last = mm(kv_ps[:, k, :], xT[a.par][:, tile(k)], wt["Wkv"][:, :], start=True, stop=True)
                    last.then_inc(kv_mm, 1)
                    need(pe, eq_rdy, a.at(1))
                    need(pe, rq_rdy, a.at(1))
                    mm(q_ps[:, :], wt["Wq"][:, :], xT[a.par][:, :], start=True, stop=True).then_inc(q_mm, 1)
                if r:
                    pe.wait_ge(x1_rdy, r.at(TT, TT))
                    need(pe, lg_rdy, r.at(1))
                    for k in range(TT):
                        last = pe.transpose(t_ps[:, tile(k)], xg[r.par][:, k, 0:D], ident[:, :])
                    last.then_inc(t_mm, 1)
                if r:
                    pe.wait_ge(x1T_rdy, r.at(1, 1))
                    for k in range(TT):
                        last = mm(t_ps[:, k * E0:(k + 1) * E0], x1T[:, tile(k)], wt["gw0"][:, :], start=True, stop=True)
                    last.then_inc(l_mm, 1)
                    need(pe, hsh_rdy, r.at(1))
                    mm(g_ps[0:I0, :], wt["sgu"][:, 0:I0], x1T[:, :], start=True, stop=True)
                    mm(u_ps[0:I0, :], wt["sgu"][:, I0:2 * I0], x1T[:, :], start=True, stop=True).then_inc(gu_mm, 1)
                if a:
                    pe.wait_ge(kf_rdy, a.at(1, 1))
                    pe.wait_ge(v_rdy, a.at(1, 1))
                    need(pe, maskT_rdy, a.at(1, -1))
                    for k in range(TT):
                        last = mm(kva_ps[:, 0:D + 1], kf[:, k, :], vext[:, k, :], start=(k == 0), stop=(k == TT - 1))
                    last.then_inc(kva_mm, 1)
                if a:
                    pe.wait_ge(kvx_rdy, a.at(1, 1))
                    pe.wait_ge(qf_rdy, a.at(1, 1))
                    for k in range(TT):
                        last = mm(o_ps[:, k, 0:D + 1], qf[:, tile(k)], kvx[:, :], start=True, stop=True)
                    last.then_inc(o_mm, 1)
                if r:
                    pe.wait_ge(hsh_rdy, r.at(1, 1))
                    need(pe, resid_rdy, r.at(1))
                    for k in range(TT):
                        last = mm(d_ps[:, tile(k)], hsh[:, tile(k)], wt["sd"][:, :], start=True, stop=True)
                    last.then_inc(d_mm, 1)
                    pe.wait_ge(route0, r.at(15, 11))
                    pe.wait_ge(kvx_rdy, a.at(1, 1) if a else NB)
                    for k in range(TT):
                        last = pe.transpose(kva_ps[0:E0, tile(k)], mask[:, k, :], ident[:, :])
                    last.then_inc(mt_mm, 1)

            stage1(Seq(0, 0), None)
            with pe.Fori(0, NB // 2 - 1) as j:
                for i in (1, 2):
                    stage1(Seq(j, i), Seq(j, i - 1))
            stage1(Seq(0, NB - 1), Seq(0, NB - 2))
            stage1(None, Seq(0, NB - 1))

            pe.wait_ge(w_loaded, W_ALL)

            pe.wait_ge(idxf_rdy, 1)
            pe.transpose(bank[6][:, 0:E0], idxf[:, :], ident[0:E0, 0:E0]).then_inc(idx_mm, 1)

            def group(s):
                pe.wait_ge(xe_got[s.par], s.half(16 * EG, 16 * EG))
                need(pe, xeT_rdy, s.at(1))
                for k in range(EG):
                    last = pe.transpose(bank[2][:, tile(k)], xe[s.par][:, k, 0:D], ident[:, :])
                last.then_inc(xeT_mm, 1)
                pe.wait_ge(xeT_rdy, s.at(1, 1))
                need(pe, ae_rdy, s.at(1))
                for k in range(EG):
                    last = mm(bank[3][:, tile(k)], xeT[:, k, :], wgu[:, bass.ds(s.at(EG, k), 1), :], start=True, stop=True)
                last.then_inc(gu_e, 1)
                pe.wait_ge(ae_rdy, s.at(1, 1))
                need(pe, aeT_rdy, s.at(1))
                settle(pe)
                for k in range(EG):
                    last = pe.transpose(bank[4][0:I0, tile(k)], ae[:, k, :], ident[:, :])
                last.then_inc(aeT_mm, 1)
                pe.wait_ge(aeT_rdy, s.at(1, 1))
                need(pe, ye_rdy, s.at(1))
                for k in range(EG):
                    last = mm(bank[5][:, tile(k)], aeT[:, k, :], wd[:, bass.ds(s.at(EG, k), 1), :], start=True, stop=True)
                last.then_inc(dn_mm, 1)

            with pe.Fori(0, E0 // EG // 2) as j:
                for i in (0, 1):
                    group(Seq(j, i))

            held = {"a": None, "v": None}

            def turn(bank_, sem_, value):
                k = "a" if bank_ is pa_ps else "v"
                if held[k]:
                    pe.wait_ge(*held[k])
                held[k] = (sem_, value)

            def front(s, n):
                if n == 3:
                    pe.wait_ge(x2_rdy, s.at(TT, TT))
                    turn(pv_ps, x2T_rdy, s.at(1, 1))
                    for k in range(TT):
                        last = pe.transpose(pv_ps[:, tile(k)], x2[s.par][:, k, :], ident[:, :])
                    last.then_inc(x2T_mm, 1)
                for h, taps in {4: ((0, range(DCONV)),), 5: ((1, range(2)),), 6: ((1, range(2, DCONV)),)}.get(n, ()):
                    if taps[0] == 0:
                        pe.wait_ge(x2T_rdy, s.at(1, 1))
                        turn(pv_ps, cv_rdy, s.at(NH, h + 1))
                    for k in taps:
                        last = mm(pv_ps[:, :], inc[:, k, tile(h)], x2T[:, k:k + SEQ], start=(k == 0), stop=(k == DCONV - 1))
                    if k == DCONV - 1:
                        last.then_inc(cv_mm, 1)
                if n in (7, 9):
                    h = (n - 7) // 2
                    turn(pa_ps, zc_rdy, s.at(NH, h + 1))
                    mm(pa_ps[:, :], wt["inp"][:, tile(NH + h)], x2T[:, DCONV - 1:], start=True, stop=True).then_inc(z_mm, 1)
                if n == 8:
                    pe.wait_ge(xc_rdy, s.at(1, 1))
                    turn(pa_ps, xpf_rdy, s.at(1, 1))
                    for k in range(TT):
                        for h in range(NH):
                            last = mm(pa_ps[:, k * NXP:(k + 1) * NXP], xc[s.par][:, h, tile(k)], wt["xpw"][:, h, :],
                                      start=(h == 0), stop=(h == NH - 1))
                    last.then_inc(xp_mm, 1)
                if n == 10:
                    pe.wait_ge(split_rdy, s.at(4, 4))
                    turn(pa_ps, parts_rdy, s.at(1, 1))
                    for k in range(TT):
                        last = mm(pa_ps[0:3 * NXP, tile(k)], xpp[:, k, :], identb[:, :], start=True, stop=True)
                    last.then_inc(parts_mm, 1)
                if n == 11:
                    pe.wait_ge(parts_rdy, s.at(1, 1))
                    turn(pa_ps, dtp_rdy, s.at(NH, NH))
                    mm(pa_ps[:, :], sel_bc[:, 0, :], parts[s.par][:, :], start=True, stop=True).then_inc(dtr_mm, 1)

            def spread_b(s, n):
                turn(pa_ps, bs_rdy, s.at(NS, n + 1))
                mm(pa_ps[:, :], sel_bc[:, 1 + n, :], parts[s.par][:, :], start=True, stop=True).then_inc(bb_rdy, 1)

            def spread_c(s, n):
                need(pe, prod_rdy, s.at(NS, n))
                mm(cb_ps[:, :], sel_bc[:, 1 + NS + n, :], parts[s.par][:, :], start=True, stop=True).then_inc(cb_rdy, 1)

            def add_state(s, n):
                if n == (1 if 0 in PAIRS else 0):
                    need(pe, yd_rdy, s.at(NH))
                if n in PAIRS:
                    return
                if n - 1 in PAIRS:
                    pe.wait_ge(pair_rdy, s.at(len(PAIRS), PAIRS.index(n - 1) + 1))
                else:
                    pe.wait_ge(prod_rdy, s.at(NS, n + 1))
                for h in range(NH):
                    last = mm(y_ps[:, h, :], ident[:, :], prod[n % 2][:, h, :], start=(sums_to(n) == 1), stop=(n == NS - 1),
                              skip_group_check=True)
                last.then_inc(y_mm, 1)

            def hidden(s, c):
                if c == 0:
                    pe.wait_ge(x3T_rdy, s.at(1, 1))
                pe.wait_ge(ha_rdy, s.at(NCH, c)) if c else None
                k = rows_of(c)
                mm(h1_ps[0:k, :], wt["w1"][:, c, 0:k], x3T[:, :], start=True, stop=True).then_inc(h1_mm, 1)
                pe.wait_ge(hg_rdy, s.at(NCH, c)) if c else None
                mm(h3_ps[0:k, :], wt["w3"][:, c, 0:k], x3T[:, :], start=True, stop=True).then_inc(h3_mm, 1)

            def spread_w(s, c):
                pe.wait_ge(rwT_rdy, s.at(1, 1))
                turn(pv_ps, hh_rdy, s.at(RT_CH, c - SH_CH + 1))
                mm(pv_ps[:, :], sel_e(c), rwTb[s.par][:, :], start=True, stop=True).then_inc(rwb_mm, 1)

            def down(s, c):
                k = rows_of(c)
                if c == 0:
                    need(pe, of_rdy, s.at(1))
                if c < SH_CH:
                    pe.wait_ge(hs_rdy, s.at(NCH, c + 1))
                else:
                    pe.wait_ge(hh_rdy, s.at(RT_CH, c - SH_CH + 1))
                h = (hs if c < SH_CH else hh)[c % 2]
                for q in range(TT):
                    last = mm(fo_ps[:, tile(q)], h[0:k, tile(q)], wt["w2"][0:k, c, :], start=(c == 0 and q == 0),
                              stop=False, skip_group_check=True)
                last.then_inc(dn_done, 1)

            def biases(s):
                for q in range(TT):
                    last = mm(fo_ps[:, tile(q)], rwT[s.par][:, tile(q)], wt["b2x"][:, :], start=False,
                              stop=True, skip_group_check=True)
                last.then_inc(b2_mm, 1)

            def out_proj(s):
                pe.wait_ge(y2_rdy, s.at(1, 1))
                turn(pv_ps, x3p_rdy, s.at(1, 1))
                for k in range(TT):
                    for h in range(NH):
                        last = mm(pv_ps[:, tile(k)], y2[:, h, tile(k)], wt["outp"][:, h, :], start=(h == 0),
                                  stop=(h == NH - 1))
                last.then_inc(op_mm, 1)

            def experts(s, n):
                if n == M0 - 1:
                    pe.wait_ge(x3_rdy, s.at(TT, TT))
                    need(pe, hg_rdy, s.at(NCH))
                    for k in range(TT):
                        last = pe.transpose(h3_ps[:, tile(k)], x3[s.par][:, k, :], ident[:, :])
                    last.then_inc(x3T_mm, 1)
                if n == M0:
                    turn(pa_ps, l1_rdy, s.at(1, 1))
                    for k in range(TT):
                        last = mm(pa_ps[:, k * E1:(k + 1) * E1], x3T[:, tile(k)], wt["gw1"][:, :], start=True, stop=True)
                    last.then_inc(l1_mm, 1)
                if n == M0 + 2:
                    pe.wait_ge(rwf_rdy, s.at(5, 5))
                    turn(pa_ps, rwT_rdy, s.at(1, 1))
                    for k in range(TT):
                        last = mm(pa_ps[0:96, tile(k)], rwp[:, k, :], identb[:, :], start=True, stop=True)
                    last.then_inc(rwT_mm, 1)

            def units(q, c, lo, hi):
                if lo <= c < hi:
                    hidden(q, c)

            def gates(q, c, lo, hi):
                if max(lo - bool(lo), SH_CH) <= c - 1 < hi - (hi < NCH):
                    spread_w(q, c - 1)

            def sums(q, c, lo, hi):
                if lo - 2 * bool(lo) <= c - 2 < hi - 2 * (hi < NCH):
                    down(q, c - 2)
                if c - 2 == NCH - 1:
                    biases(q)

            def iteration(f, s, m, o, ahead):
                if o:
                    held["v"] = (hh_rdy, o.at(RT_CH, NS - M0 - 1 - SH_CH))
                if s:
                    held["a"] = (bs_rdy, s.at(NS, 2))
                for n in range(NS):
                    of_o = (NS + n - M0, NS - M0, NCH)
                    of_m = (n - M0, 0, NS - M0)
                    if s:
                        spread_c(s, n)
                    if m and n == 0:
                        add_state(m, NS - 1)
                    if m and n < M0:
                        experts(m, n)
                    if s and n:
                        add_state(s, n - 1)
                    if s and n < NS - 2:
                        spread_b(s, n + 2)
                    if f and n >= NS - 2:
                        spread_b(f, n + 2 - NS)
                    if o:
                        units(o, *of_o)
                    if m:
                        units(m, *of_m)
                    if m and n >= M0:
                        experts(m, n)
                    if f and n not in LATE:
                        front(f, n)
                    if o:
                        gates(o, *of_o)
                    if m:
                        gates(m, *of_m)
                    if o:
                        sums(o, *of_o)
                    if m:
                        sums(m, *of_m)
                    if f and n in LATE:
                        front(f, n)
                    if m and n == 1:
                        out_proj(m)

            pe.wait_ge(added, E0 // 2 * 16)
            pe.wait_ge(added2, E0 // 2 * 16)
            pe.wait_ge(const_rdy, N_CONST)
            pe.wait_ge(half_rdy, 6 + DCONV)
            schedule(pe, iteration)

        @block.vector
        def _(dve):
            tt, ts, stt = dve.tensor_tensor, dve.tensor_scalar, dve.scalar_tensor_tensor

            def spread(a, shape):
                return a.to_broadcast(shape)

            dve.memset(zero[:, :], 0.0).then_inc(dve_init, 1)
            dve.memset(vext[:, :, D:D + 1], 1.0).then_inc(dve_init, 1)
            def halve(*weights):
                for w in weights:
                    ts(w, w, 0.5, None, ALU.mult).then_inc(half_rdy, 1)

            dve.wait_ge(w_early, 16 * len(EARLY))
            halve(wt["sgu"][:, 0:I0])
            dve.wait_ge(const_rdy, N_EARLY)

            def stats_of(src, st, m, s, done):
                for k in range(TT):
                    dve.bn_stats(st[:, k, :], src[:, k, :]).then_inc(done, 1)
                dve.wait_ge(done, s.at(8, 4))
                settle(dve)
                for k in range(TT):
                    dve.bn_aggr(m[:, k, :], st[:, k, :]).then_inc(done, 1)

            def normalise(dst, src, m, r, s, ready, done):
                dve.wait_ge(ready, s.at(2, 2))
                for k in range(TT):
                    ts(dst[:, k, 0:D], src[:, k, :], m[:, k, 0:1], r[:, k:k + 1], ALU.subtract, ALU.mult).then_inc(done, 1)

            def one_hot(dst, index, k, width):
                a = iota_e[:, 0:width].rearrange("p (a b e) -> p a b e", a=1, b=1)
                b = index[:, :, 0:k].rearrange("p t (k e) -> p t k e", e=1)
                return tt(dst[:, :, :, :], a.to_broadcast([P, TT, k, width]), b.to_broadcast([P, TT, k, width]), ALU.is_equal)

            def col(a, width):
                return a[:, :].rearrange("p (t e) -> p t e", e=1).to_broadcast([P, TT, width])

            def stage1(a, r):
                if a:
                    dve.wait_ge(v_rdy, a.at(1, 1))
                    ts(rk[:, :, :], kv_ps[:, :, 0:D], 0.0, 1.0, ALU.max, ALU.add).then_inc(rk_rdy, 1)
                    dve.wait_ge(eq_rdy, a.at(1, 1))
                    ts(rq[:, :], q_ps[:, :], 0.0, 1.0, ALU.max, ALU.add).then_inc(rq_rdy, 1)
                    dve.wait_ge(rk_rdy, a.at(1, 1))
                    need(dve, kva_mm, a.at(1))
                    tt(kf[:, :, :], ek[:, :, :], rk[:, :, :], ALU.min).then_inc(kf_rdy, 1)
                    dve.wait_ge(rq_rdy, a.at(1, 1))
                    need(dve, o_mm, a.at(1))
                    tt(qf[:, :], eq[:, :], rq[:, :], ALU.min).then_inc(qf_rdy, 1)
                if r:
                    dve.wait_ge(lg_rdy, r.at(1, 1))
                    settle(dve)
                    for k in range(TT):
                        dve.max(top[:, k, :], lg[:, k, :]).then_inc(route0, 1)
                    dve.wait_ge(route0, r.at(15, 4))
                    tt(lsub[:, :, :], lg[:, :, :], top[:, :, 0:1].to_broadcast([P, TT, E0]), ALU.subtract).then_inc(route0, 1)
                    for k in range(TT):
                        dve.max_index(topi[:, k, :], top[:, k, :], lg[:, k, :]).then_inc(route0, 1)
                    dve.wait_ge(tg_rdy, r.at(1, 1))
                    stt(sg[:, :], tg[:, :], 1.0, g_ps[0:I0, :], ALU.add, ALU.mult).then_inc(sg_rdy, 1)
                    dve.wait_ge(route0, r.at(15, 9))
                    one_hot(hot, topi, TOPK, E0).then_inc(route0, 1)
                    dve.wait_ge(sg_rdy, r.at(1, 1))
                    need(dve, d_mm, r.at(1))
                    tt(hsh[:, :], sg[:, :], u_ps[0:I0, :], ALU.mult).then_inc(hsh_rdy, 1)
                    dve.wait_ge(route0, r.at(15, 10))
                    need(dve, mt_mm, r.at(1))
                    dve.tensor_reduce(mask[:, :, :], hot[:, :, :, :].rearrange("p t k e -> p t e k"), AX.X, ALU.add
                                      ).then_inc(route0, 1)
                if a:
                    dve.wait_ge(o_mm, a.at(1, 1))
                    ts(den[:, :], o_ps[:, :, D], Z_EPS, None, ALU.add).then_inc(den_rdy, 1)
                    dve.wait_ge(den_rdy, a.at(1, 1))
                    dve.reciprocal(rz[:, :], den[:, :]).then_inc(rz_rdy, 1)
                if r:
                    dve.wait_ge(route0, r.at(15, 11))
                    dve.wait_ge(lexp_rdy, r.at(1, 1))
                    tt(gm[:, :, :], lexp[:, :, :], mask[:, :, :], ALU.mult).then_inc(route0, 1)
                if a:
                    dve.wait_ge(rz_rdy, a.at(1, 1))
                    dve.wait_ge(ldx[a.par], a.half(32, 32))
                    for k in range(TT):
                        stt(pre[:, k, :], o_ps[:, k, 0:D], rz[:, k:k + 1], xt[a.par][:, k, :], ALU.mult, ALU.add
                            ).then_inc(pre_rdy, 1)
                    dve.wait_ge(pre_rdy, a.at(TT, TT))
                    stats_of(pre, stats, mv, a, mv_rdy)
                if r:
                    dve.wait_ge(route0, r.at(15, 12))
                    dve.tensor_reduce(gs[:, :], gm[:, :, :], AX.X, ALU.add).then_inc(route0, 1)
                    dve.wait_ge(route0, r.at(15, 13))
                    dve.reciprocal(gr[:, :], gs[:, :]).then_inc(route0, 1)
                    dve.wait_ge(route0, r.at(15, 14))
                    tt(xg[r.par][:, :, D:XGW], gm[:, :, :], col(gr, E0), ALU.mult).then_inc(route0, 1)
                    dve.wait_ge(d_mm, r.at(1, 1))
                    need(dve, st_r, r.at(16))
                    tt(resid[:, :, :], blk4(d_ps), xg[r.par][:, :, 0:D], ALU.add).then_inc(resid_rdy, 1)
                if a:
                    need(dve, st_xg[a.par], a.half(16))
                    need(dve, t_mm, a.at(1, -1))
                    normalise(xg[a.par], pre, mv, rstd, a, rstd_rdy, x1_rdy)

            stage1(Seq(0, 0), None)
            with dve.Fori(0, NB // 2 - 1) as j:
                for i in (1, 2):
                    stage1(Seq(j, i), Seq(j, i - 1))
            stage1(Seq(0, NB - 1), Seq(0, NB - 2))
            stage1(None, Seq(0, NB - 1))

            def take(src, dst, got):
                for c in range(CAP // 8):
                    got_c = dst[:, c * 8:(c + 1) * 8]
                    if c:
                        dve.wait_ge(taken, take_n[0])
                    dve.max(got_c, src).then_inc(got, 1)
                    dve.wait_ge(got, c + 1)
                    if c < CAP // 8 - 1:
                        dve.match_replace(src, got_c, src, 0.0).then_inc(taken, 1)
                        take_n[0] += 1

            take_n = [0]
            dve.wait_ge(seg_loaded, 16 * NSEG)
            tt(val[:, :], val[:, :], rev[:, :], ALU.mult).then_inc(val_rdy, 1)
            dve.wait_ge(val_rdy, 1)
            take(val[:, :], cand, cand_rdy)
            dve.wait_ge(cand_loaded, 16 * NSEG)
            take(cval[:, :], first, first_rdy)
            stt(empty[:, :], first[:, :], 0.0, slot_no[:, :], ALU.is_equal, ALU.mult).then_inc(empty_rdy, 1)
            dve.wait_ge(empty_rdy, 1)
            tt(idxf[:, :], empty[:, :], first[:, :], ALU.subtract).then_inc(idxd_rdy, 1)
            dve.wait_ge(idxd_rdy, 1)
            ts(idxf[:, :], idxf[:, :], float(TOK), None, ALU.add).then_inc(idxf_rdy, 1)
            dve.wait_ge(idx_mm, 1)
            dve.tensor_copy(idx[:, :], bank[6][:, 0:E0]).then_inc(idx_rdy, 1)

            def group(s):
                dve.wait_ge(te_rdy, s.at(1, 1))
                stt(se[:, :, :], te[:, :, :], 1.0, blk4(bank[3])[:, :, 0:I0], ALU.add, ALU.mult).then_inc(se_rdy, 1)
                dve.wait_ge(xe_got[s.par], s.half(16 * EG, 16 * EG))
                need(dve, ye_rdy, s.at(1))
                for k in range(EG):
                    dve.tensor_copy(ge[:, k:k + 1], xe[s.par][:, k, bass.ds(s.at(EG, D + k), 1)]).then_inc(ge_rdy, 1)
                dve.wait_ge(se_rdy, s.at(1, 1))
                need(dve, aeT_mm, s.at(1))
                stt(ae[:, :, :], se[:, :, :], 0.5, blk4(bank[3])[:, :, I0:2 * I0], ALU.mult, ALU.mult).then_inc(ae_rdy, 1)
                dve.wait_ge(dn_mm, s.at(1, 1))
                dve.wait_ge(ge_rdy, s.at(EG, EG))
                for done in (added, added2):
                    need(dve, done, s.at(8 * EG, -8 * EG))
                tt(ye[s.par][:, :, :], blk4(bank[5]), ge[:, :].rearrange("p (k e) -> p k e", e=1).to_broadcast([P, EG, D]),
                   ALU.mult).then_inc(ye_rdy, 1)

            dve.wait_ge(w_loaded, W_ALL)
            halve(wt["inp"][:, DI:2 * DI], convw[:, :, :], wt["convb"][:, :], wt["w1"][:, :, :], wt["b1"][:, :])
            dve.wait_ge(half_rdy, 6)
            for k in range(DCONV):
                tt(inc[:, k, :], wt["inp"][:, 0:DI], convw[:, k, :], ALU.mult).then_inc(half_rdy, 1)
            dve.wait_ge(a_exp, 1)
            ts(aneg[:, :, :], aneg[:, :, :], -1.0, None, ALU.mult).then_inc(a_neg, 1)

            group(Seq(0, 0))
            group(Seq(0, 1))
            with dve.Fori(1, E0 // EG // 2) as j:
                for i in (0, 1):
                    group(Seq(j, i))

            def front(s, n):
                if n == 2:
                    need(dve, x3p_rdy, s.at(1, -1))
                    normalise(x2[s.par], rin, mv1, rs1, s, f_rs, x2_rdy)
                if n in (8, 10):
                    h = (n - 8) // 2
                    dve.wait_ge(zc_rdy, s.at(NH, h + 1))
                    need(dve, y2_rdy, s.at(1, -1))
                    stt(zs[s.par][:, h, :], tz[:, h, :], 1.0, zc[:, h, :], ALU.add, ALU.mult).then_inc(zs_rdy, 1)
                if n == 7:
                    dve.wait_ge(cv_rdy, s.at(NH, NH))
                    need(dve, yd_rdy, s.at(NH, -NH))
                    stt(xc[s.par][:, :, :], tc[:, :, :], 1.0, cv[:, :, :], ALU.add, ALU.mult).then_inc(xc_rdy, 1)
                if n == 9:
                    part = [xpp[:, :, k * NXP:(k + 1) * NXP] for k in range(3)]
                    dve.wait_ge(xpf_rdy, s.at(1, 1))
                    need(dve, parts_mm, s.at(1))
                    dve.tensor_copy(part[0], xpf[:, :, :]).then_inc(split_rdy, 1)
                    dve.wait_ge(split_rdy, s.at(4, 1))
                    tt(xpr[:, :, :], xpf[:, :, :], part[0], ALU.subtract).then_inc(split_rdy, 1)
                    dve.wait_ge(split_rdy, s.at(4, 2))
                    dve.tensor_copy(part[1], xpr[:, :, :]).then_inc(split_rdy, 1)
                    dve.wait_ge(split_rdy, s.at(4, 3))
                    tt(part[2], xpr[:, :, :], part[1], ALU.subtract).then_inc(split_rdy, 1)

            def stats_ahead(s):
                dve.wait_ge(ld_r2, s.at(16, 16))
                stats_of(rin, st1, mv1, s, f_mv)

            def softplus(s):
                dve.wait_ge(dtl_rdy, s.at(1, 1))
                need(dve, da_rdy, s.at(NS * NH, -NS * NH))
                need(dve, u_rdy, s.at(1, -1))
                stt(dt_[s.par][:, :, :], dtp[:, :, :], 0.0, dta[:, :, :], ALU.max, ALU.add).then_inc(dt_rdy, 1)

            over_h = lambda b: b[:, :].rearrange("p (h t) -> p h t", h=1).to_broadcast([P, NH, SEQ])
            flat = lambda a: a[:, :, :].rearrange("p h t -> p (h t)")

            def gate(s, c):
                k = rows_of(c)
                dve.wait_ge(ha_rdy, s.at(NCH, c + 1))
                dve.wait_ge(h3_mm, s.at(NCH, c + 1))
                stt(hg[c % 2][0:k, :], h3_ps[0:k, :], wt["b3"][0:k, c:c + 1], ha[0:k, :], ALU.add, ALU.mult).then_inc(hg_rdy, 1)

            def silu(s, c):
                k = rows_of(c)
                dve.wait_ge(ht_rdy, s.at(NCH, c + 1))
                if c in (2, 3):
                    dve.wait_ge(dn_done, s.at(NCH, c - 1))
                stt(hs[c % 2][0:k, :], ht[c % 2][0:k, :], 1.0, hg[c % 2][0:k, :], ALU.add, ALU.mult).then_inc(hs_rdy, 1)

            def weigh(s, c):
                dve.wait_ge(hs_rdy, s.at(NCH, c + 1))
                dve.wait_ge(rwb_mm, s.at(RT_CH, c - SH_CH + 1))
                dve.wait_ge(dn_done, s.at(NCH, c - 1))
                tt(hh[c % 2][:, :], hs[c % 2][:, :], pv_ps[:, :], ALU.mult).then_inc(hh_rdy, 1)

            def experts(s, n):
                if n == 0:
                    dve.wait_ge(y_mm, s.at(NADD, NADD))
                    need(dve, y2_rdy, s.at(1))
                    for h in range(NH):
                        stt(yd[:, h, :], xc[s.par][:, h, :], wt["dskip"][:, h:h + 1], y_ps[:, h, :], ALU.mult, ALU.add
                            ).then_inc(yd_rdy, 1)
                if n == 2:
                    dve.wait_ge(op_mm, s.at(1, 1))
                    tt(x3p[:, :, :], blk4(pv_ps), x2[s.par][:, :, :], ALU.add).then_inc(x3p_rdy, 1)
                    dve.wait_ge(x3p_rdy, s.at(1, 1))
                    stats_of(x3p, st2, mv2, s, m_mv)
                if n == 3:
                    normalise(x3[s.par], x3p, mv2, rs2, s, m_rs, x3_rdy)
                if n == M0:
                    dve.wait_ge(l1_rdy, s.at(1, 1))
                    dve.tensor_reduce(l1m[:, :], l1[:, :, :], AX.X, ALU.max).then_inc(route1, 1)
                    dve.wait_ge(route1, s.at(16, 1))
                    tt(l1s[:, :, :], l1[:, :, :], col(l1m, E1), ALU.subtract).then_inc(route1, 1)
                if n == M0 + 1:
                    dve.wait_ge(l1e_rdy, s.at(1, 1))
                    dve.tensor_reduce(l1z[:, :], l1e[:, :, :], AX.X, ALU.add).then_inc(route1, 1)
                    dve.wait_ge(route1, s.at(16, 3))
                    dve.reciprocal(l1r[:, :], l1z[:, :]).then_inc(route1, 1)
                    dve.wait_ge(route1, s.at(16, 4))
                    tt(sc1[:, :, :], l1e[:, :, :], col(l1r, E1), ALU.mult).then_inc(route1, 1)
                    dve.wait_ge(route1, s.at(16, 5))
                    tt(bi1[:, :, :], sc1[:, :, :], wt["gb1"][:, :].rearrange("p (t e) -> p t e", t=1).to_broadcast([P, TT, E1]),
                       ALU.add).then_inc(route1, 1)
                    dve.wait_ge(route1, s.at(16, 6))
                    settle(dve)
                    for k in range(TT):
                        dve.max(tp1[:, k, :], bi1[:, k, :]).then_inc(route1, 1)
                    dve.wait_ge(route1, s.at(16, 10))
                    settle(dve)
                    for k in range(TT):
                        dve.max_index(ti1[:, k, :], tp1[:, k, :], bi1[:, k, :]).then_inc(route1, 1)
                    dve.wait_ge(route1, s.at(16, 14))
                    one_hot(ho1, ti1, 2, E1).then_inc(route1, 1)
                    dve.wait_ge(route1, s.at(16, 15))
                    tt(hm1[:, :, :], ho1[:, :, 0, :], ho1[:, :, 1, :], ALU.add).then_inc(route1, 1)
                    dve.wait_ge(route1, s.at(16, 16))
                    need(dve, rwf_rdy, s.at(5))
                    tt(rw[:, :, 0:E1], sc1[:, :, :], hm1[:, :, :], ALU.mult).then_inc(rwf_rdy, 1)
            def tail(s, n):
                if n == TAIL + 2:
                    dve.wait_ge(b2_mm, s.at(1, 1))
                    tt(of[:, :, :], blk4(fo_ps), x3[s.par][:, :, :], ALU.add).then_inc(of_rdy, 1)
                    dve.wait_ge(of_rdy, s.at(1, 1))
                    stats_of(of, st3, mv3, s, o_mv)
                if n == TAIL + 3:
                    need(dve, st_o, s.at(16))
                    normalise(ofin, of, mv3, rs3, s, o_rs, ofin_rdy)

            def iteration(f, s, m, o, ahead):
                for n in range(NS):
                    c = n - M0
                    co = NS + n - M0
                    if s:
                        dve.wait_ge(dbx_rdy, s.at(NS, n + 1))
                        dve.wait_ge(da_rdy, s.at(NS * NH, NH * (n + 1)))
                        need(dve, prod_rdy, s.at(NS, n - 1))
                        dve.tensor_tensor_scan(flat(hst[n % 2]), flat(dA[n % 2]), flat(dbx[n % 2]), 0.0, ALU.mult, ALU.add
                                               ).then_inc(scan_rdy, 1)
                    if m and c >= 1:
                        silu(m, c - 1)
                    if o and co - 1 < NCH:
                        silu(o, co - 1)
                    if s:
                        dve.wait_ge(scan_rdy, s.at(NS, n + 1))
                        dve.wait_ge(cb_rdy, s.at(NS, n + 1))
                        if n - 2 in PAIRS:
                            dve.wait_ge(pair_rdy, s.at(len(PAIRS), PAIRS.index(n - 2) + 1))
                        else:
                            need(dve, y_mm, s.at(NADD, sums_to(n - 2) if n > 1 else n - 1))
                        tt(prod[n % 2][:, :, :], hst[n % 2][:, :, :], over_h(cb_ps), ALU.mult).then_inc(prod_rdy, 1)
                    if f and n == NS - 2:
                        softplus(f)
                    if s and n - 1 in PAIRS:
                        dve.wait_ge(prod_rdy, s.at(NS, n + 1))
                        tt(prod[n % 2][:, :, :], prod[0][:, :, :], prod[1][:, :, :], ALU.add).then_inc(pair_rdy, 1)
                    if o and co < NCH:
                        gate(o, co)
                    if m and c >= 0:
                        gate(m, c)
                    if m:
                        experts(m, n)
                    if m and c - 1 >= SH_CH:
                        weigh(m, c - 1)
                    if o and co - 1 < NCH:
                        weigh(o, co - 1)
                    if o:
                        tail(o, n)
                    if f:
                        front(f, n)
                    if ahead and n == NS - 1:
                        stats_ahead(ahead)

            dve.wait_ge(added, E0 // 2 * 16)
            dve.wait_ge(added2, E0 // 2 * 16)
            dve.memset(rw[:, :, E1:E1 + 1], 1.0)
            dve.memset(rwp[:, :, :], 0.0)
            dve.tensor_copy(identb[:, :], ident[:, :])
            dve.memset(x2T[:, 0:DCONV - 1], 0.0)
            for k in range(2):
                dve.memset(dA[k][:, :, 0:1], 0.0).then_inc(dve_init, 1)
            dve.wait_ge(dve_init, 4)
            stats_ahead(Seq(0, 0))
            schedule(dve, iteration)


def kernel(**inputs):
    import numpy as np
    import concourse.bacc as bacc
    from concourse.bass_utils import run_bass_kernel_spmd

    g = {k: np.asarray(v) for k, v in inputs.items()}
    c = np.ascontiguousarray

    def halves(a):
        return c(np.moveaxis(a.reshape(NH, P, *a.shape[1:]), 0, 1))

    def chunks(shared, routed):
        pad = np.zeros((D, SH_CH * P - H1), np.float32)
        return c(np.concatenate([shared, pad, np.moveaxis(routed, 0, 1).reshape(D, -1)], 1).reshape(D, NCH, P))

    def bias_chunks(shared, routed):
        pad = np.zeros(SH_CH * P - H1, np.float32)
        return c(np.concatenate([shared, pad, routed.reshape(-1)]).reshape(NCH, P).T)

    x = g["L0_attn_x"].reshape(TOK, D)
    W = g["L0_attn_W"]
    xp = g["L1_attn_x_proj_w"]
    w2 = np.concatenate([g["L1_ffn_sw2"], np.zeros((SH_CH * P - H1, D), np.float32), g["L1_ffn_w2"].reshape(-1, D)], 0)
    t = {
        "x": x, "xT": c(x.T), "Wq": c(W[:, :D]), "Wkv": c(W[:, D:]), "gw0": c(g["L0_ffn_gate_w"].T),
        "wgu": c(np.moveaxis(g["L0_ffn_w_gate_up"], 0, 1)), "wd": c(np.moveaxis(g["L0_ffn_w_down"], 0, 1)),
        "sgu": g["L0_ffn_shared_w_gate_up"], "sd": g["L0_ffn_shared_w_down"],
        "inp": c(g["L1_attn_in_proj_w"].T), "convw": c(np.broadcast_to(g["L1_attn_conv_w"][:, 0].T[None], (P, DCONV, DI))), "convb": halves(g["L1_attn_conv_b"]),
        "xpw": halves(xp.T),
        "dtw": halves(g["L1_attn_dt_proj_w"][:, 0]), "dtb": halves(g["L1_attn_dt_proj_b"]),
        "alog": halves(g["L1_attn_A_log"]), "dskip": halves(g["L1_attn_D"]), "outp": halves(g["L1_attn_out_proj_w"].T),
        "gw1": c(g["L1_ffn_gate_w"].T), "gb1": c(np.broadcast_to(g["L1_ffn_gate_b"], (P, E1))),
        "w1": chunks(g["L1_ffn_sw1"], g["L1_ffn_w1"]), "w3": chunks(g["L1_ffn_sw3"], g["L1_ffn_w3"]),
        "b1": bias_chunks(g["L1_ffn_sb1"], g["L1_ffn_b1"]), "b3": bias_chunks(g["L1_ffn_sb3"], g["L1_ffn_b3"]),
        "w2": c(np.moveaxis(w2.reshape(NCH, P, D), 0, 1)),
        "b2x": c(np.tile(np.concatenate([g["L1_ffn_b2"], g["L1_ffn_sb2"][None], np.zeros((31 - E1, D), np.float32)], 0), (3, 1))),
    }
    nc = bacc.Bacc("TRN2", target_bir_lowering=False, num_devices=1)
    arrays = {f"in_{n}": c(a) for n, a in t.items()}
    ins = {n: nc.dram_tensor(f"in_{n}", a.shape, F32, kind="ExternalInput").ap() for n, a in t.items()}
    out = nc.dram_tensor("out_dram", (TOK, D), F32, kind="ExternalOutput").ap()
    build(nc, ins, out)
    r = run_bass_kernel_spmd(nc, [arrays], core_ids=[0])
    return r.results[0]["out_dram"].reshape(NB, SEQ, D)
```
